# Optimizing a Trainium2 kernel written in Bass

```python
import numpy as np
import jax
import jax.numpy as jnp

def _softmax(x, axis=-1):
    return jax.nn.softmax(x, axis=axis)

def _gelu(x):
    return jax.nn.gelu(x, approximate=True)

def _silu(x):
    return jax.nn.silu(x)

def _sigmoid(x):
    return jax.nn.sigmoid(x)

def _layernorm(x, axis=-1, eps=1e-05):
    m = jnp.mean(x, axis=axis, keepdims=True)
    v = jnp.var(x, axis=axis, keepdims=True)
    return (x - m) / jnp.sqrt(v + eps)

def _scatter_add(tgt, idx, src, axis=0):
    return tgt.at[idx].add(src)

def _segment_sum(src, seg, n):
    return jax.ops.segment_sum(src, seg, n)
kernel_name = 'mk_flamingo_gated_d1_seqx_r8_33b8e8'

def setup_inputs(seed: int=0):
    np.random.seed(seed)
    _w = jnp.asarray

    def _rec_inputs():
        import jax
        import jax.numpy as jnp
        _rk = jax.random.key(seed)
        x = 0.0002417 + 0.9998 * jax.random.normal(jax.random.fold_in(_rk, 1), (32, 128, 128), jnp.float32)
        _lenS = 128 - jax.random.randint(jax.random.fold_in(_rk, 7), (32,), 0, max(1, 128 // 4) + 1, jnp.int32)
        _lenS2 = 128 - jax.random.randint(jax.random.fold_in(_rk, 8), (32,), 0, max(1, 128 // 4) + 1, jnp.int32)
        _ctx_1024P = jax.random.normal(jax.random.fold_in(_rk, 11), (32, 16, 128), jnp.float32)
        _ctx_1024c = jax.random.dirichlet(jax.random.fold_in(_rk, 511), 0.3 * jnp.ones((16,), jnp.float32), (32, 128))
        _ctx_1024t = jnp.einsum('bsk,bkd->bsd', _ctx_1024c, _ctx_1024P)
        _ctx_1024t = _ctx_1024t * jax.lax.rsqrt(jnp.mean(jnp.square(_ctx_1024t)) + 1e-12) * 0.953939
        ctx_1024 = 7.22013e-05 + 1.00017 * (_ctx_1024t + 0.3 * jax.random.normal(jax.random.fold_in(_rk, 611), (32, 128, 128), jnp.float32))
        _g = jax.random.normal(jax.random.fold_in(_rk, 9001), (2, 1), jnp.float32)
        _g = jnp.sign(_g) * jnp.maximum(jnp.abs(_g), 1.0) + (_g == 0) * 1.0
        g_xattn = _g[0]
        g_ffn = _g[1]
        return (x, ctx_1024, g_xattn, g_ffn)
    x, ctx_1024, g_xattn, g_ffn = _rec_inputs()

    def _L0_xattn_setup():
        import jax, jax.numpy as jnp
        import numpy as np
        EMBED_SIZE = 128
        HEADS = 16
        HEAD_DIM = EMBED_SIZE // HEADS
        key = jax.random.key(seed)
        k1, k2, k3, k4 = jax.random.split(key, 4)
        N, L = (4, 256)
        return {'values': jax.random.normal(k1, (N, L, EMBED_SIZE), dtype=jnp.float32), 'keys': jax.random.normal(k2, (N, L, EMBED_SIZE), dtype=jnp.float32), 'query': jax.random.normal(k3, (N, L, EMBED_SIZE), dtype=jnp.float32), 'w_out': jax.random.normal(k4, (EMBED_SIZE, EMBED_SIZE), dtype=jnp.float32) * (1.0 / np.sqrt(EMBED_SIZE)), 'b_out': jnp.zeros((EMBED_SIZE,), dtype=jnp.float32)}
    _L0_xattn_all = _L0_xattn_setup()
    _L0_xattn_in = {k: v for k, v in _L0_xattn_all.items() if k in ('w_out', 'b_out')}
    del _L0_xattn_all

    def _L0_ffn_setup():
        import jax, jax.numpy as jnp
        import numpy as np
        B, S, D, F, E, K = (2, 256, 128, 512, 8, 2)
        key = jax.random.key(seed)
        ks = jax.random.split(key, 5)
        x = jax.random.normal(ks[0], (B, S, D), dtype=jnp.float32)
        Wg = jax.random.normal(ks[1], (D, E), dtype=jnp.float32) * 0.02
        W1 = jax.random.normal(ks[2], (E, D, F), dtype=jnp.float32) * 0.02
        b1 = jnp.zeros((E, F), dtype=jnp.float32)
        W2 = jax.random.normal(ks[3], (E, F, D), dtype=jnp.float32) * 0.02
        b2 = jnp.zeros((E, D), dtype=jnp.float32)
        return {'x': x, 'Wg': Wg, 'W1': W1, 'b1': b1, 'W2': W2, 'b2': b2}
    _L0_ffn_all = _L0_ffn_setup()
    _L0_ffn_in = {k: v for k, v in _L0_ffn_all.items() if k in ('Wg', 'W1', 'b1', 'W2', 'b2')}
    del _L0_ffn_all
    return {'x': x, 'ctx_1024': ctx_1024, 'g_xattn': g_xattn, 'g_ffn': g_ffn, 'L0_xattn_w_out': _L0_xattn_in['w_out'], 'L0_xattn_b_out': _L0_xattn_in['b_out'], 'L0_ffn_Wg': _L0_ffn_in['Wg'], 'L0_ffn_W1': _L0_ffn_in['W1'], 'L0_ffn_b1': _L0_ffn_in['b1'], 'L0_ffn_W2': _L0_ffn_in['W2'], 'L0_ffn_b2': _L0_ffn_in['b2']}

def reference(x, ctx_1024, g_xattn, g_ffn, L0_xattn_w_out, L0_xattn_b_out, L0_ffn_Wg, L0_ffn_W1, L0_ffn_b1, L0_ffn_W2, L0_ffn_b2):
    import jax
    import jax.numpy as jnp

    def _L0_xattn_ref(values, keys, query, w_out, b_out):
        import jax, jax.numpy as jnp
        import numpy as np
        EMBED_SIZE = 128
        HEADS = 16
        HEAD_DIM = EMBED_SIZE // HEADS
        N, q_len, _ = query.shape
        v_len = values.shape[1]
        k_len = keys.shape[1]
        v = values.reshape(N, v_len, HEADS, HEAD_DIM)
        k = keys.reshape(N, k_len, HEADS, HEAD_DIM)
        q = query.reshape(N, q_len, HEADS, HEAD_DIM)
        energy = jnp.einsum('nqhd,nkhd->nhqk', q, k)
        attn = jax.nn.softmax(energy / jnp.sqrt(jnp.float32(EMBED_SIZE)), axis=3)
        out = jnp.einsum('nhql,nlhd->nqhd', attn, v).reshape(N, q_len, EMBED_SIZE)
        return out @ w_out.T + b_out

    def _L0_ffn_ref(x, Wg, W1, b1, W2, b2):
        import jax, jax.numpy as jnp
        import numpy as np
        B, S, D, F, E, K = (2, 256, 128, 512, 8, 2)
        b, s, d = x.shape
        e = Wg.shape[1]
        T = b * s
        C = 2 * K * T // e
        xt = x.reshape(T, d)
        logits = xt.astype(jnp.float32) @ Wg.astype(jnp.float32)
        gates = jax.nn.softmax(logits, axis=-1)
        idx1 = jnp.argmax(gates, axis=-1)
        mask1 = jax.nn.one_hot(idx1, e, dtype=gates.dtype)
        gate1 = jnp.sum(gates * mask1, axis=-1)
        logits2 = jnp.where(mask1 > 0, -jnp.inf, logits)
        idx2 = jnp.argmax(logits2, axis=-1)
        mask2 = jax.nn.one_hot(idx2, e, dtype=gates.dtype)
        gate2 = jnp.sum(gates * mask2, axis=-1)
        denom = gate1 + gate2 + 1e-09
        w1 = gate1 / denom
        w2 = gate2 / denom
        p1 = jnp.cumsum(mask1, axis=0) - mask1
        pos1 = jnp.sum(p1 * mask1, axis=-1).astype(jnp.int32)
        off = jnp.sum(mask1, axis=0)
        p2 = jnp.cumsum(mask2, axis=0) - mask2 + off[None, :]
        pos2 = jnp.sum(p2 * mask2, axis=-1).astype(jnp.int32)
        keep1 = (pos1 < C).astype(xt.dtype)
        keep2 = (pos2 < C).astype(xt.dtype)
        pos1 = jnp.clip(pos1, 0, C - 1)
        pos2 = jnp.clip(pos2, 0, C - 1)
        xe = jnp.zeros((e, C, d), dtype=xt.dtype)
        xe = xe.at[idx1, pos1].add(xt * keep1[:, None])
        xe = xe.at[idx2, pos2].add(xt * keep2[:, None])
        h = jax.nn.gelu(jnp.einsum('ecd,edf->ecf', xe, W1) + b1[:, None, :], approximate=False)
        ye = jnp.einsum('ecf,efd->ecd', h, W2) + b2[:, None, :]
        out = ye[idx1, pos1] * (w1 * keep1)[:, None] + ye[idx2, pos2] * (w2 * keep2)[:, None]
        return out.reshape(b, s, d)
    x = x + jnp.tanh(g_xattn[0]) * _L0_xattn_ref(ctx_1024, ctx_1024, _layernorm(x, axis=-1), L0_xattn_w_out, L0_xattn_b_out)
    x = x + jnp.tanh(g_ffn[0]) * _L0_ffn_ref(_layernorm(x, axis=-1), L0_ffn_Wg, L0_ffn_W1, L0_ffn_b1, L0_ffn_W2, L0_ffn_b2)
    return x

_drawn_inputs = setup_inputs


def setup_inputs(seed=0):
    import zlib

    import numpy as np

    out = dict(_drawn_inputs(seed))
    spreads = {'L0_xattn_b_out': (0.0, 0.1), 'L0_ffn_b1': (0.0, 0.542), 'L0_ffn_b2': (0.0, 0.1)}
    factors = {}
    for name, (base, spread) in spreads.items():
        noise = np.random.default_rng([zlib.crc32(name.encode()), seed]).standard_normal(out[name].shape)
        drawn = base * np.exp(spread * noise) if base else spread * noise
        out[name] = jnp.asarray(drawn.astype(out[name].dtype))
    for name, factor in factors.items():
        out[name] = (out[name] * factor).astype(out[name].dtype)
    return out
```

```python
from collections import namedtuple
from contextlib import ExitStack

import concourse.bass as bass
from concourse import mybir

F32 = mybir.dt.float32
BF16 = mybir.dt.bfloat16
I32 = mybir.dt.int32
U32 = mybir.dt.uint32
ALU = mybir.AluOpType
ACT = mybir.ActivationFunctionType
AX = mybir.AxisListType

P = 128
HD = 8
LN_EPS = 1e-5
GATE_EPS = 1e-9

Seq = namedtuple("Seq", "pair slot")


def flamingo_layer(nc, x, ctx, g_xattn, g_ffn, w_out, b_out, Wg, W1, b1, W2, b2, out):
    B, S, D = x.shape
    E = Wg.shape[1]
    FF = W1.shape[2]
    T = B * S
    K = 2
    CAP = 2 * K * T // E
    H = D // HD
    G = 4
    J = H // G
    SCALE = 1.0 / float(D) ** 0.5
    NF = FF // P
    MID = T
    REGION = 2 * T + P
    PAD_ROW = E * REGION
    NT = 72
    assert NT % 4 == 0 and NT * P > K * T + (E - 1) * (P - 1) and S == P and D == P
    ROW = D + 1
    CH = 4
    NC = B // CH

    xs_dram = nc.dram_tensor("expert_rows", [PAD_ROW + P, ROW], F32, kind="Internal").ap()
    y_dram = nc.dram_tensor("choice_rows", [K * T, D], F32, kind="Internal").ap()

    with ExitStack() as es:
        def sb(name, shape, dt=F32):
            return es.enter_context(nc.sbuf_tensor(name, shape, dt))

        def sem(name):
            return es.enter_context(nc.semaphore(name))

        bank = [es.enter_context(nc.psum_tensor(f"bank{i}", [P, 512], F32)) for i in range(8)]

        col_i = sb("col_i", [P, P], I32)
        row_i = sb("row_i", [P, P], I32)
        diff_i = sb("diff_i", [P, P], I32)
        head_of_row = sb("head_of_row", [P, P], I32)
        head_of_col = sb("head_of_col", [P, P], I32)
        ident = sb("ident", [P, P])
        ident_b = sb("ident_b", [P, P], BF16)
        before = sb("before", [P, P], BF16)
        ones_b = sb("ones_b", [P, P], BF16)
        row_mask = sb("row_mask", [P, J, P])
        row_mask_b = sb("row_mask_b", [P, J, P], BF16)
        col_mask = sb("col_mask", [P, J, D])
        neg_half = sb("neg_half", [P, 1])
        iota8 = sb("iota8", [P, 8])
        ids = sb("ids", [P, B, 2], I32)
        pos_sign = sb("pos_sign", [P, 2])
        pos_base = sb("pos_base", [P, 2])
        zeros = sb("zeros", [P, 1024])
        pad = sb("pad", [P, ROW])
        wout_sb = sb("wout_sb", [P, D])
        woutT = sb("woutT", [P, D])
        bias_out = sb("bias_out", [P, D])
        gates = sb("gates", [P, 2])
        tanh_g = sb("tanh_g", [P, 2])
        wg_sb = sb("wg_sb", [P, E])
        ED = FF + D + NF
        ex_sb = sb("ex_sb", [P, E, ED])
        w2_sb = sb("w2_sb", [P, E * NF * D])
        b1_rows = sb("b1_rows", [E * NF, P])
        x_all = sb("x_all", [P, B * D])
        ctx_s = sb("ctx_s", [P, 2, D])
        st1 = sb("st1", [P, 2, 6])
        mv1 = sb("mv1", [P, 2, 2])
        ve1 = sb("ve1", [P, 2])
        rstd1 = sb("rstd1", [P, 2])
        st2 = sb("st2", [P, 2, 6])
        mv2 = sb("mv2", [P, 2, 2])
        ve2 = sb("ve2", [P, 2])
        rstd2 = sb("rstd2", [P, 2])
        xn = sb("xn", [P, 2, D])
        qm = sb("qm", [P, 2, J, P])
        qmb = sb("qmb", [P, 2, J, P], BF16)
        kT = sb("kT", [P, 2, P])
        kTb = sb("kTb", [P, 2, P], BF16)
        vm = sb("vm", [P, 2, J, D])
        negmax = sb("negmax", [P, 2, H, HD], BF16)
        mT = sb("mT", [P, 2, P], BF16)
        probs = sb("probs", [P, 2, G, J * P])
        rsum = sb("rsum", [P, P])
        aT = sb("aT", [P, 2, P])
        xrow = sb("xrow", [P, 2, 2, ROW])
        xn2T = sb("xn2T", [P, 2, P])
        lg = sb("lg", [P, 2, E])
        top = sb("top", [P, 2, 8])
        topi = sb("topi", [P, 2, 8], U32)
        idxf = sb("idxf", [P, 2, 2])
        chosen = sb("chosen", [P, 2, 2, E], BF16)
        carry = sb("carry", [P, 2, 2 * E])
        place = sb("place", [P, 2, E])
        place2 = sb("place2", [P, 2, E])
        pos = sb("pos", [P, 2])
        pos2 = sb("pos2", [P, 2])
        pos3 = sb("pos3", [P, 2])
        slot_i = sb("slot_i", [P, 2, 2], U32)
        top_all = sb("top_all", [P, B, 8])
        tdiff = sb("tdiff", [P, B, 8])
        texp = sb("texp", [P, B, 8])
        gsum = sb("gsum", [P, B])
        gden = sb("gden", [P, B])
        gden2 = sb("gden2", [P, B])
        gw = sb("gw", [P, 2, B])
        grec = sb("grec", [P, B])
        n_first = sb("n_first", [1, E])
        n_room = sb("n_room", [1, E])
        n_second = sb("n_second", [1, E])
        n_kept = sb("n_kept", [1, E])
        nt_i = sb("nt_i", [1, E], I32)
        nt_sh = sb("nt_sh", [1, E], I32)
        nt_f = sb("nt_f", [1, E])
        pair_i = sb("pair_i", [1, E, E], I32)
        earlier = sb("earlier", [1, E, E])
        t_mul = sb("t_mul", [1, E, E])
        t_first = sb("t_first", [1, E])
        t_end = sb("t_end", [1, E])
        region_i = sb("region_i", [1, E])
        r_start = sb("r_start", [1, E])
        r_off = sb("r_off", [1, E])
        r_step = sb("r_step", [1, E])
        tile_i = sb("tile_i", [1, NT])
        past = sb("past", [1, NT, E])
        past_step = sb("past_step", [1, NT, E])
        tile_e = sb("tile_e", [1, NT])
        tile_r = sb("tile_r", [1, NT])
        tile_r2 = sb("tile_r2", [1, NT])
        tile_r3 = sb("tile_r3", [1, NT])
        tile_r4 = sb("tile_r4", [1, NT])
        expert_tab = sb("expert_tab", [1, NT], I32)
        row_tab = sb("row_tab", [1, NT], I32)
        pad_tab = sb("pad_tab", [1, E], I32)
        xt = sb("xt", [P, 4, ROW])
        dest = sb("dest", [P, 4, 1], U32)
        xtT = sb("xtT", [P, 2, P])
        ex_cur = sb("ex_cur", [P, 4, ED])
        hT = sb("hT", [P, 2, NF, P])
        y_s = sb("y_s", [P, 4, D])
        yc = sb("yc", [P, 2, B, D])

        S_BANK, E_BANK = bank[0:2], bank[2:4]
        TA, TB, O_BANK, R_BANK = bank[4], bank[5], bank[6], bank[7]
        TB_max = TB[:, 256:256 + P // 2].bitcast(BF16)
        X_BANK, H_BANK, Y_BANK = bank[0:2], bank[2:4], bank[4:6]

        iota_done, const_done, chain = sem("iota_done"), sem("const_done"), sem("chain")
        pool_const = sem("pool_const")
        gate_loaded, w_loaded, x_loaded, moe_loaded = sem("gate_loaded"), sem("w_loaded"), sem("x_loaded"), sem("moe_loaded")
        tanh_done, woutT_psum, b1T_psum, prep_done = sem("tanh_done"), sem("woutT_psum"), sem("b1T_psum"), sem("prep_done")
        zeroed = sem("zeroed")
        ctx_loaded = [sem(f"ctx_loaded{u}") for u in range(2)]
        ln1_stats, ln1_aggr, ln1_var, ln1_rstd, xn_ready = sem("ln1_stats"), sem("ln1_aggr"), sem("ln1_var"), sem("ln1_rstd"), sem("xn_ready")
        xb_done = sem("xb_done")
        xnT_ready, ctxT_ready, qm_ready, qmb_ready = sem("xnT_ready"), sem("ctxT_ready"), sem("qm_ready"), sem("qmb_ready")
        kT_ready, vm_ready = sem("kT_ready"), sem("vm_ready")
        s_ready, max_done, m_psum, mT_ready = sem("s_ready"), sem("max_done"), sem("m_psum"), sem("mT_ready")
        e_ready, exp_done, o_ready = sem("e_ready"), sem("exp_done"), sem("o_ready")
        rsum_done, aT_ready, proj_ready = sem("rsum_done"), sem("aT_ready"), sem("proj_ready")
        x1_done, ln2_stats, ln2_aggr, ln2_var, ln2_rstd = sem("x1_done"), sem("ln2_stats"), sem("ln2_aggr"), sem("ln2_var"), sem("ln2_rstd")
        xn2_ready, xn2T_psum, xn2T_ready = sem("xn2_ready"), sem("xn2T_psum"), sem("xn2T_ready")
        logit_ready, lg_done, chosen_done = sem("logit_ready"), sem("lg_done"), sem("chosen_done")
        top_max, top_idx, top_num = sem("top_max"), sem("top_idx"), sem("top_num")
        cum_ready, slot_done = sem("cum_ready"), sem("slot_done")
        place_done, carry_done, picked, pos_summed, pos_signed, pos_based = [
            sem(s) for s in ("place_done", "carry_done", "picked", "pos_summed", "pos_signed", "pos_based")]
        row_out = [sem(f"row_out{u}") for u in range(2)]
        gexp_ready, gexp_done, gw_step = sem("gexp_ready"), sem("gexp_done"), sem("gw_step")
        table_step, table_done, pads_out = sem("table_step"), sem("table_done"), sem("pads_out")
        xt_loaded = [sem(f"xt_loaded{v}") for v in range(4)]
        xt_psum, xtT_ready, ex_ready, dest_ready = sem("xt_psum"), sem("xtT_ready"), sem("ex_ready"), sem("dest_ready")
        h_psum, hT_ready, y_psum = sem("h_psum"), sem("hT_ready"), sem("y_psum")
        y_ready = [sem(f"y_ready{v}") for v in range(4)]
        y_out = [sem(f"y_out{v}") for v in range(4)]
        yc_loaded = [sem(f"yc_loaded{k}") for k in range(NC)]
        fin_step, fin_done = sem("fin_step"), sem("fin_done")
        stored = sem("stored")

        def at(s, scale=1, plus=0):
            return s.pair * (2 * scale) + (s.slot * scale + plus)

        def wait(eng, semaphore, value):
            if isinstance(value, int) and value < 1:
                return
            eng.wait_ge(semaphore, value)

        def wait_alone(eng, semaphore, value):
            eng.wait_ge(const_done, 1)
            eng.wait_ge(semaphore, value)

        def cols(s, width=P):
            return bass.ds(at(s, width), width) if not isinstance(s.pair, int) else slice(at(s, width), at(s, width) + width)

        def pipeline(eng, step):
            def due(t):
                return [Seq(k // 2, k % 2) if 0 <= k < B else None for k in (t + 1, t, t - 1, t - 2, t - 3)]

            FIRST, LAST = 4, 32
            for t in range(-1, FIRST):
                step(*due(t))
            with eng.Fori(FIRST // 2, LAST // 2 - 1) as i:
                for u in range(2):
                    step(*[Seq(i + (u + k) // 2, (u + k) % 2) for k in (1, 0, -1, -2, -3)])
            for t in range(LAST - 2, B + 3):
                step(*due(t))

        def tiles(eng, early, front, back):
            NI = NT // 4

            def turn(i, v, ahead):
                for part, k in ((early, 2), (front, 1), (back, 0)):
                    if v + k < 4 or ahead:
                        part(i + (v + k) // 4, (v + k) % 4)

            early(0, 0)
            early(0, 1)
            front(0, 0)
            for v in range(4):
                turn(0, v, True)
            with eng.Fori(1, NI - 1) as i:
                for v in range(4):
                    turn(i, v, True)
            for v in range(4):
                turn(NI - 1, v, False)

        block = es.enter_context(nc.Block())

        @block.sync
        def _(sp):
            xv = x.rearrange("b s d -> s b d")
            xa = x_all[:, :].rearrange("p (b d) -> p b d", b=B)
            sp.dma_start(xa[:, 0:2, :], xv[:, 0:2, :]).then_inc(x_loaded, 16)
            for u in range(2):
                sp.dma_start(ctx_s[:, u, :], ctx[u]).then_inc(ctx_loaded[u], 16)
            sp.dma_start(gates[:, 0:1], g_xattn.partition_broadcast(P)).then_inc(gate_loaded, 16)
            sp.dma_start(gates[:, 1:2], g_ffn.partition_broadcast(P)).then_inc(gate_loaded, 16)
            sp.dma_start(wout_sb[:, :], w_out).then_inc(w_loaded, 16)
            sp.dma_start(bias_out[:, :], b_out.partition_broadcast(P)).then_inc(w_loaded, 16)
            sp.dma_start(b1_rows[:, :], b1.rearrange("e (c f) -> (e c) f", c=NF)).then_inc(w_loaded, 16)
            sp.dma_start(wg_sb[:, :], Wg).then_inc(w_loaded, 16)
            sp.dma_start(xa[:, 2:8, :], xv[:, 2:8, :]).then_inc(x_loaded, 16)
            for k in range(1, 4):
                sp.dma_start(xa[:, 8 * k:8 * k + 8, :], xv[:, 8 * k:8 * k + 8, :]).then_inc(x_loaded, 16)
            sp.dma_start(ex_sb[:, :, 0:FF], W1.rearrange("e d f -> d e f")).then_inc(moe_loaded, 16)
            sp.dma_start(w2_sb[:, :].rearrange("p (e c d) -> p e c d", e=E, c=NF),
                         W2.rearrange("e (c f) d -> f e c d", c=NF)).then_inc(moe_loaded, 16)
            sp.dma_start(ex_sb[:, :, FF:FF + D], b2.partition_broadcast(P)).then_inc(moe_loaded, 16)
            sp.wait_ge(pool_const, 1)
            zrows = y_dram[0:K * T, :].rearrange("(k p r) d -> k p (r d)", p=P, r=8)
            for k in range(K * T // (8 * P)):
                sp.dma_start(zrows[k], zeros[:, :]).then_inc(zeroed, 16)

            def load_ctx(s):
                wait(sp, ctxT_ready, at(s, 1, -1))
                wait(sp, vm_ready, at(s, 1, -1))
                sp.dma_start(ctx_s[:, s.slot, :], ctx[at(s)]).then_inc(ctx_loaded[s.slot], 16)

            with sp.Fori(1, B // 2) as i:
                for u in range(2):
                    load_ctx(Seq(i, u))

            sp.wait_ge(table_done, 1)
            for u in range(2):
                sp.wait_ge(row_out[u], 16 * B)
            for e in range(E):
                r = sp.value_load(pad_tab[0:1, e:e + 1], min_val=0, max_val=PAD_ROW)
                sp.dma_start(xs_dram[bass.ds(r, P), :], pad[:, :]).then_inc(pads_out, 16)
            sp.dma_start(xs_dram[PAD_ROW:PAD_ROW + P, :], pad[:, :]).then_inc(pads_out, 16)
            sp.wait_ge(pads_out, 16 * (E + 1))

            def load_tile(i, v):
                t = i * 4 + v
                wait(sp, xt_psum, t - 3)
                wait(sp, dest_ready, t - 3)
                r = sp.value_load(row_tab[0:1, bass.ds(t, 1)], min_val=0, max_val=PAD_ROW)
                sp.dma_start(xt[:, v, :], xs_dram[bass.ds(r, P), :]).then_inc(xt_loaded[v], 16)

            for v in range(4):
                load_tile(0, v)
            with sp.Fori(1, NT // 4) as i:
                for v in range(4):
                    load_tile(i, v)

            for v in range(4):
                sp.wait_ge(y_out[v], 16 * (NT // 4))
            yv = y_dram[0:K * T, :].rearrange("(c b p) d -> c p b d", c=K, p=P)
            for k in range(NC):
                for c in range(K):
                    sp.dma_start(yc[:, c, CH * k:CH * k + CH, :], yv[c, :, CH * k:CH * k + CH, :]).then_inc(yc_loaded[k], 16)
            ov = out.rearrange("b s d -> s b d")
            for k in range(NC):
                sp.wait_ge(fin_done, CH * (k + 1))
                sp.dma_start(ov[:, CH * k:CH * k + CH, :], xa[:, CH * k:CH * k + CH, :]).then_inc(stored, 16)
            sp.wait_ge(stored, 16 * NC)

        @block.gpsimd
        def _(pool):
            nc.gpsimd.iota(col_i[:, :], [[1, P]], base=0, channel_multiplier=0)
            nc.gpsimd.iota(row_i[:, :], [[0, P]], base=0, channel_multiplier=1)
            nc.gpsimd.iota(diff_i[:, :], [[1, P]], base=0, channel_multiplier=-1)
            nc.gpsimd.iota(ids[:, :, :], [[P, B], [T, 2]], base=0, channel_multiplier=1)
            nc.gpsimd.iota(pair_i[:, :, :], [[-1, E], [1, E]], base=0, channel_multiplier=0)
            nc.gpsimd.iota(region_i[:, :], [[REGION, E]], base=MID, channel_multiplier=0, allow_small_or_imprecise_dtypes=True)
            nc.gpsimd.iota(tile_i[:, :], [[1, NT]], base=0, channel_multiplier=0, allow_small_or_imprecise_dtypes=True)
            nc.gpsimd.iota(pad[:, D:D + 1].bitcast(I32), [[0, 1]], base=K * T, channel_multiplier=1)
            nc.gpsimd.memset(pad[:, 0:D], 0.0)
            nc.gpsimd.memset(ones_b[:, :], 1.0)
            nc.gpsimd.memset(neg_half[:, :], -0.5)
            nc.gpsimd.memset(carry[:, 1, :], 0.0)
            nc.gpsimd.memset(pos_sign[:, 0:1], 1.0)
            nc.gpsimd.memset(pos_sign[:, 1:2], -1.0)
            nc.gpsimd.memset(pos_base[:, 0:1], float(MID))
            nc.gpsimd.memset(pos_base[:, 1:2], float(MID - 1))
            nc.gpsimd.memset(negmax[:, :, :, :], 0.0).then_inc(iota_done, 1)
            nc.gpsimd.memset(zeros[:, :], 0.0).then_inc(pool_const, 1)

            def step(n, a, b, c, d):
                if c:
                    pool.wait_ge(ln2_var, at(c, 1, 1))
                    nc.gpsimd.tensor_tensor(rstd2[:, c.slot:c.slot + 1], ve2[:, c.slot:c.slot + 1], neg_half[:, :],
                                            ALU.pow).then_inc(ln2_rstd, 1)
                if n:
                    pool.wait_ge(ln1_var, at(n, 1, 1))
                    nc.gpsimd.tensor_tensor(rstd1[:, n.slot:n.slot + 1], ve1[:, n.slot:n.slot + 1], neg_half[:, :],
                                            ALU.pow).then_inc(ln1_rstd, 1)
                if a:
                    if isinstance(a.pair, int) and a == Seq(0, 0):
                        pool.wait_ge(prep_done, 3)
                        pool.wait_ge(const_done, 1)
                    wait(pool, ctx_loaded[a.slot], a.pair * 16 + 16)
                    wait(pool, o_ready, at(a, 1, -1))
                    nc.gpsimd.tensor_tensor(vm[:, a.slot, :, :], ctx_s[:, a.slot, :].unsqueeze(1).to_broadcast([P, J, D]),
                                            col_mask[:, :, :], ALU.mult).then_inc(vm_ready, 1)
                    pool.wait_ge(xn_ready, at(a, 1, 1))
                    if d:
                        pool.wait_ge(slot_done, at(d, 1, 1))
                    nc.gpsimd.tensor_tensor(x_all[:, cols(a)], x_all[:, cols(a)], bias_out[:, :], ALU.add).then_inc(xb_done, 1)
                if d:
                    if not a:
                        pool.wait_ge(slot_done, at(d, 1, 1))
                    for k in range(2):
                        nc.gpsimd.indirect_dma_start(
                            xs_dram, bass.IndirectOffsetOnAxis(ap=slot_i[:, d.slot, k:k + 1], axis=0),
                            xrow[:, d.slot, k, :], None).then_inc(row_out[d.slot], 16)

            pipeline(pool, step)

            pool.wait_ge(zeroed, 16 * (K * T // (8 * P)))

            last_row = pool.snap(K * T - 1)
            with pool.Fori(1, NT // 4 + 1) as i:
                for v in range(4):
                    wait_alone(pool, y_ready[v], i)
                    nc.gpsimd.indirect_dma_start(y_dram, bass.IndirectOffsetOnAxis(ap=dest[:, v, :], axis=0), y_s[:, v, :],
                                                 None, bounds_check=last_row, oob_is_err=False).then_inc(y_out[v], 16)

        @block.scalar
        def _(act):
            act.wait_ge(gate_loaded, 32)
            nc.scalar.activation(tanh_g[:, :], gates[:, :], ACT.Tanh).then_inc(tanh_done, 1)

            def step(n, a, b, c, d):
                if a:
                    act.wait_ge(ctxT_ready, at(a, 1, 1))
                    nc.scalar.copy(kT[:, a.slot, :], TB[:, 0:P]).then_inc(kT_ready, 1)
                    nc.scalar.copy(kTb[:, a.slot, :], TB[:, 0:P]).then_inc(kT_ready, 1)

                def exp(g):
                    act.wait_ge(e_ready, at(b, G, g + 1))
                    if g == 0:
                        wait(act, o_ready, at(b, 1, -1))
                    nc.scalar.activation(probs[:, b.slot, g, :], E_BANK[g % 2][:, :], ACT.Exp,
                                         scale=SCALE).then_inc(exp_done, 1)

                if b:
                    exp(0)
                    exp(1)
                if c:
                    act.wait_ge(xn2T_psum, at(c, 1, 1))
                    wait(act, logit_ready, at(c, 1, -1))
                    nc.scalar.copy(xn2T[:, c.slot, :], TB[:, P:2 * P]).then_inc(xn2T_ready, 1)
                if b:
                    exp(2)
                    exp(3)
                if a:
                    act.wait_ge(m_psum, at(a, 1, 1))
                    nc.scalar.copy(mT[:, a.slot, :], TB_max).then_inc(mT_ready, 1)

            pipeline(act, step)

            act.wait_ge(gexp_ready, 1)
            nc.scalar.activation(texp[:, :, :], tdiff[:, :, :], ACT.Exp).then_inc(gexp_done, 1)

            def gelu(i, v):
                t = i * 4 + v
                act.wait_ge(h_psum, t + 1)
                wait(act, y_psum, t - 1)
                for c in range(NF):
                    last = nc.scalar.activation(hT[:, v % 2, c, :], H_BANK[v % 2][:, c * P:c * P + P], ACT.Gelu,
                                                bias=ex_cur[:, v, FF + D + c:FF + D + c + 1])
                last.then_inc(hT_ready, 1)

            for v in range(4):
                gelu(0, v)
            with act.Fori(1, NT // 4) as i:
                for v in range(4):
                    gelu(i, v)

        @block.tensor
        def _(pe):
            pe.wait_ge(const_done, 1)
            pe.wait_ge(w_loaded, 64)
            nc.tensor.transpose(TA[:, 0:P], wout_sb[:, :], ident[:, :]).then_inc(woutT_psum, 1)
            nc.tensor.transpose(TB[:, 0:E * NF], b1_rows[:, :], ident[0:E * NF, 0:E * NF]).then_inc(b1T_psum, 1)
            pe.wait_ge(prep_done, 3)

            def free_TB(n_kT, n_xn2T, n_mT):
                wait(pe, kT_ready, n_kT)
                wait(pe, xn2T_ready, n_xn2T)
                wait(pe, mT_ready, n_mT)

            def step(n, a, b, c, d):
                if c:
                    pe.wait_ge(aT_ready, at(c, 1, 1))
                    wait(pe, slot_done, at(c))
                    nc.tensor.matmul(R_BANK[:, 0:D], aT[:, c.slot, :], woutT[:, :], start=True, stop=True).then_inc(proj_ready, 1)
                if a:
                    pe.wait_ge(xn_ready, at(a, 1, 1))
                    wait(pe, qm_ready, at(a))
                    nc.tensor.transpose(TA[:, 0:P], xn[:, a.slot, :], ident[:, :]).then_inc(xnT_ready, 1)
                    pe.wait_ge(ctx_loaded[a.slot], a.pair * 16 + 16)
                    free_TB(0, at(c) if c else 0, at(a))
                    nc.tensor.transpose(TB[:, 0:P], ctx_s[:, a.slot, :], ident[:, :]).then_inc(ctxT_ready, 1)

                def main_scores(g):
                    wait(pe, exp_done, at(b, G, g - 1))
                    r = slice(32 * g, 32 * g + 32)
                    acc = E_BANK[g % 2]
                    nc.tensor.matmul(acc[:, :], kT[r, b.slot, :], qm[r, b.slot, :, :], start=True, stop=False,
                                     skip_group_check=True)
                    if g == 0:
                        pe.wait_ge(mT_ready, at(b, 1, 1))
                    for j in range(J):
                        last = nc.tensor.matmul(acc[:, j * P:j * P + P], row_mask_b[r, j, :], mT[r, b.slot, :],
                                                start=False, stop=True, skip_group_check=True)
                    last.then_inc(e_ready, 1)

                def max_scores(g):
                    wait(pe, max_done, at(a, G, g - 1))
                    if g == 0:
                        pe.wait_ge(qmb_ready, at(a, 1, 1))
                        pe.wait_ge(kT_ready, at(a, 2, 2))
                    r = slice(32 * g, 32 * g + 32)
                    for j in range(J):
                        last = nc.tensor.matmul(S_BANK[g % 2][:, j * P:j * P + P], qmb[r, a.slot, j, :], kTb[r, a.slot, :],
                                                start=True, stop=True)
                    last.then_inc(s_ready, 1)

                if b:
                    main_scores(0)
                    main_scores(1)
                if a:
                    max_scores(0)
                    max_scores(1)
                if c:
                    pe.wait_ge(xn2_ready, at(c, 1, 1))
                    free_TB(at(a, 2, 2) if a else 2 * B, 0, at(a) if a else B)
                    nc.tensor.transpose(TB[:, P:2 * P], xrow[:, c.slot, 0, 0:D], ident[:, :]).then_inc(xn2T_psum, 1)
                if b:
                    main_scores(2)
                    main_scores(3)
                if a:
                    max_scores(2)
                    max_scores(3)
                if c:
                    pe.wait_ge(xn2T_ready, at(c, 1, 1))
                    pe.wait_ge(x1_done, at(c, 1, 1))
                    nc.tensor.matmul(R_BANK[:, P:P + E], xn2T[:, c.slot, :], wg_sb[:, :], start=True, stop=True).then_inc(logit_ready, 1)
                if b:
                    pe.wait_ge(exp_done, at(b, G, G))
                    pe.wait_ge(vm_ready, at(b, 1, 1))
                    wait(pe, aT_ready, at(b))
                    for j in range(J):
                        for lhs, o in ((vm[:, b.slot, j, :], 0), (col_mask[:, j, :], P)):
                            for g in range(G):
                                r = slice(32 * g, 32 * g + 32)
                                last = nc.tensor.matmul(O_BANK[r, o:o + P], lhs[:, r], probs[:, b.slot, g, j * P:j * P + P],
                                                        start=(j == 0 and o == 0), stop=(j == J - 1), skip_group_check=True)
                    last.then_inc(o_ready, 1)
                if a:
                    pe.wait_ge(max_done, at(a, G, G))
                    free_TB(at(a, 2, 2), at(c, 1, 1) if c else 0, at(a))
                    nc.tensor.transpose(TB_max, negmax[:, a.slot, :, :].rearrange("p h d -> p (h d)"), ident_b[:, :]).then_inc(m_psum, 1)
                if c:
                    pe.wait_ge(chosen_done, at(c, 1, 1))
                    pe.wait_ge(lg_done, at(c, 1, 1))
                    pick = chosen[:, c.slot, :, :].rearrange("p k e -> p (k e)")
                    nc.tensor.matmul(R_BANK[:, 192:192 + 2 * E], before[:, :], pick, start=True, stop=True)
                    nc.tensor.matmul(R_BANK[:, 224:224 + 2 * E], ones_b[:, :], pick, start=True, stop=True).then_inc(cum_ready, 1)

            pipeline(pe, step)

            pe.wait_ge(table_done, 1)
            pe.wait_ge(moe_loaded, 48)

            def early(i, v):
                t = i * 4 + v
                pe.wait_ge(xt_loaded[v], i * 16 + 16)
                wait(pe, xtT_ready, t - 1)
                nc.tensor.transpose(X_BANK[v % 2][:, 0:P], xt[:, v, 0:D], ident[:, :]).then_inc(xt_psum, 1)

            def front(i, v):
                t = i * 4 + v
                pe.wait_ge(xtT_ready, t + 1)
                pe.wait_ge(ex_ready, t + 1)
                wait(pe, hT_ready, t - 1)
                for c in range(NF):
                    last = nc.tensor.matmul(H_BANK[v % 2][:, c * P:c * P + P], ex_cur[:, v, c * P:c * P + P],
                                            xtT[:, v % 2, :], start=True, stop=True)
                last.then_inc(h_psum, 1)

            def back(i, v):
                t = i * 4 + v
                e = pe.value_load(expert_tab[0:1, bass.ds(t, 1)], min_val=0, max_val=E - 1)
                pe.wait_ge(hT_ready, t + 1)
                if v >= 2:
                    pe.wait_ge(y_ready[v - 2], i + 1)
                else:
                    wait(pe, y_ready[v + 2], i)
                for c in range(NF):
                    last = nc.tensor.matmul(Y_BANK[v % 2][:, 0:D], hT[:, v % 2, c, :],
                                            w2_sb[:, bass.ds(e * (NF * D) + c * D, D)], start=(c == 0), stop=(c == NF - 1))
                last.then_inc(y_psum, 1)

            tiles(pe, early, front, back)

        @block.vector
        def _(dve):
            links = [0]

            def link(ins):
                links[0] += 1
                ins.then_inc(chain, 1)
                dve.wait_ge(chain, links[0])

            dve.wait_ge(iota_done, 1)
            V = nc.vector
            V.tensor_scalar(ident[:, :], diff_i[:, :], 0.0, None, ALU.is_equal)
            V.tensor_scalar(ident_b[:, :], diff_i[:, :], 0.0, None, ALU.is_equal)
            V.tensor_scalar(before[:, :], diff_i[:, :], 0.0, None, ALU.is_gt)
            V.tensor_copy(iota8[:, :], col_i[:, 0:8])
            V.tensor_scalar(earlier[:, :, :], pair_i[:, :, :], 0.0, None, ALU.is_lt)
            V.tensor_scalar(head_of_row[:, :], row_i[:, :], 3, 3, ALU.logical_shift_right, ALU.bitwise_and)
            link(V.tensor_scalar(head_of_col[:, :], col_i[:, :], 3, 3, ALU.logical_shift_right, ALU.bitwise_and))
            for j in range(J):
                V.tensor_scalar(row_mask[:, j, :], head_of_row[:, :], float(j), None, ALU.is_equal)
                V.tensor_scalar(row_mask_b[:, j, :], head_of_row[:, :], float(j), None, ALU.is_equal)
                last = V.tensor_scalar(col_mask[:, j, :], head_of_col[:, :], float(j), None, ALU.is_equal)
            last.then_inc(const_done, 1)
            dve.wait_ge(const_done, 1)
            dve.wait_ge(tanh_done, 1)
            dve.wait_ge(woutT_psum, 1)
            V.tensor_scalar(woutT[:, :], TA[:, 0:P], tanh_g[:, 0:1], None, ALU.mult).then_inc(prep_done, 1)
            V.tensor_scalar(bias_out[:, :], bias_out[:, :], tanh_g[:, 0:1], None, ALU.mult).then_inc(prep_done, 1)
            dve.wait_ge(b1T_psum, 1)
            V.tensor_copy(ex_sb[:, :, FF + D:ED], TB[:, 0:E * NF].rearrange("p (e c) -> p e c", e=E)).then_inc(prep_done, 1)

            def ln_aggr(mv, st, ve, u, aggr_sem, count, var_sem):
                V.bn_aggr(mv[:, u, :], st[:, u, :]).then_inc(aggr_sem, 1)
                dve.wait_ge(aggr_sem, count)
                V.tensor_scalar(ve[:, u:u + 1], mv[:, u, 1:2], LN_EPS, None, ALU.add).then_inc(var_sem, 1)

            def step(n, a, b, c, d):
                if c:
                    u = c.slot
                    dve.wait_ge(proj_ready, at(c, 1, 1))
                    dve.wait_ge(xb_done, at(c, 1, 1))
                    V.tensor_tensor(x_all[:, cols(c)], R_BANK[:, 0:D], x_all[:, cols(c)], ALU.add).then_inc(x1_done, 1)
                    wait_alone(dve, x1_done, at(c, 1, 1))
                    V.bn_stats(st2[:, u, :], x_all[:, cols(c)]).then_inc(ln2_stats, 1)
                    wait_alone(dve, ln2_stats, at(c, 1, 1))
                    ln_aggr(mv2, st2, ve2, u, ln2_aggr, at(c, 1, 1), ln2_var)
                if n:
                    if isinstance(n.pair, int) and n == Seq(0, 0):
                        dve.wait_ge(x_loaded, 16 * 5)
                    V.bn_stats(st1[:, n.slot, :], x_all[:, cols(n)]).then_inc(ln1_stats, 1)
                if a:
                    u = a.slot
                    dve.wait_ge(xnT_ready, at(a, 1, 1))
                    wait(dve, e_ready, at(a, G, -G))
                    V.tensor_tensor(qm[:, u, :, :], TA[:, 0:P].unsqueeze(1).to_broadcast([P, J, P]), row_mask[:, :, :],
                                    ALU.mult).then_inc(qm_ready, 1)
                    dve.wait_ge(qm_ready, at(a, 1, 1))
                    if n:
                        dve.wait_ge(ln1_stats, at(n, 1, 1))
                    V.tensor_copy(qmb[:, u, :, :], qm[:, u, :, :]).then_inc(qmb_ready, 1)
                if n:
                    if not a:
                        dve.wait_ge(ln1_stats, at(n, 1, 1))
                    ln_aggr(mv1, st1, ve1, n.slot, ln1_aggr, at(n, 1, 1), ln1_var)
                if c:
                    u = c.slot
                    dve.wait_ge(ln2_rstd, at(c, 1, 1))
                    wait(dve, row_out[u], c.pair * 32)
                    V.tensor_copy(xrow[:, u, :, D:D + 1].bitcast(I32), ids[:, bass.ds(at(c), 1), :].rearrange("p b k -> p (b k)").unsqueeze(2))
                    V.tensor_scalar(xrow[:, u, :, 0:D], x_all[:, cols(c)].unsqueeze(1).to_broadcast([P, 2, D]), mv2[:, u, 0:1],
                                    rstd2[:, u:u + 1], ALU.subtract, ALU.mult).then_inc(xn2_ready, 1)
                if a:
                    for g in range(G):
                        dve.wait_ge(s_ready, at(a, G, g + 1))
                        if g == 0:
                            wait(dve, m_psum, at(a, 1, -1))
                        V.tensor_reduce(negmax[:, a.slot, J * g:J * g + J, 0], S_BANK[g % 2][:, :].rearrange("p (j k) -> p j k", j=J),
                                        AX.X, ALU.max, negate=True).then_inc(max_done, 1)
                if c:
                    u = c.slot
                    dve.wait_ge(logit_ready, at(c, 1, 1))
                    V.tensor_copy(lg[:, u, :], R_BANK[:, P:P + E]).then_inc(lg_done, 1)
                    wait_alone(dve, lg_done, at(c, 1, 1))
                    V.max(top[:, u, :], lg[:, u, :]).then_inc(top_max, 1)
                    wait_alone(dve, top_max, at(c, 1, 1))
                    V.max_index(topi[:, u, :], top[:, u, :], lg[:, u, :]).then_inc(top_idx, 1)
                    V.tensor_copy(top_all[:, bass.ds(at(c), 1), :], top[:, u, :].unsqueeze(1))
                    dve.wait_ge(top_idx, at(c, 1, 1))
                    V.tensor_copy(idxf[:, u, :], topi[:, u, 0:2]).then_inc(top_num, 1)
                    dve.wait_ge(top_num, at(c, 1, 1))
                    V.tensor_tensor(chosen[:, u, :, :], iota8[:, :].unsqueeze(1).to_broadcast([P, 2, E]),
                                    idxf[:, u, :].unsqueeze(2).to_broadcast([P, 2, E]), ALU.is_equal).then_inc(chosen_done, 1)
                if b:
                    u = b.slot
                    dve.wait_ge(o_ready, at(b, 1, 1))
                    V.reciprocal(rsum[:, :], O_BANK[:, P:2 * P]).then_inc(rsum_done, 1)
                    dve.wait_ge(rsum_done, at(b, 1, 1))
                    wait(dve, proj_ready, at(b, 1, -1))
                    V.tensor_tensor(aT[:, u, :], O_BANK[:, 0:P], rsum[:, :], ALU.mult).then_inc(aT_ready, 1)
                if c:
                    u = c.slot
                    dve.wait_ge(cum_ready, at(c, 1, 1))
                    wait(dve, carry_done, at(c))
                    V.tensor_tensor(place[:, :, :].rearrange("p k e -> p (k e)"), R_BANK[:, 192:192 + 2 * E], carry[:, 1 - u, :], ALU.add).then_inc(place_done, 1)
                    V.tensor_tensor(carry[:, u, :], R_BANK[:, 224:224 + 2 * E], carry[:, 1 - u, :], ALU.add).then_inc(carry_done, 1)
                    dve.wait_ge(place_done, at(c, 1, 1))
                    V.tensor_tensor(place2[:, :, :], place[:, :, :], chosen[:, u, :, :], ALU.mult).then_inc(picked, 1)
                    dve.wait_ge(picked, at(c, 1, 1))
                    V.tensor_reduce(pos[:, :], place2[:, :, :], AX.X, ALU.add).then_inc(pos_summed, 1)
                    dve.wait_ge(pos_summed, at(c, 1, 1))
                    V.tensor_tensor(pos2[:, :], pos[:, :], pos_sign[:, :], ALU.mult).then_inc(pos_signed, 1)
                    dve.wait_ge(pos_signed, at(c, 1, 1))
                    V.tensor_tensor(pos3[:, :], pos2[:, :], pos_base[:, :], ALU.add).then_inc(pos_based, 1)
                    dve.wait_ge(pos_based, at(c, 1, 1))
                    V.scalar_tensor_tensor(out=slot_i[:, u, :], in0=idxf[:, u, :], scalar=float(REGION), in1=pos3[:, :],
                                           op0=ALU.mult, op1=ALU.add).then_inc(slot_done, 1)
                if n:
                    u = n.slot
                    dve.wait_ge(ln1_rstd, at(n, 1, 1))
                    wait(dve, xnT_ready, at(n, 1, -1))
                    V.tensor_scalar(xn[:, u, :], x_all[:, cols(n)], mv1[:, u, 0:1], rstd1[:, u:u + 1],
                                    ALU.subtract, ALU.mult).then_inc(xn_ready, 1)

            pipeline(dve, step)

            dve.wait_ge(carry_done, B)
            last_carry = carry[0:1, (B - 1) % 2, :]
            link(V.tensor_scalar(n_first[:, :], last_carry[:, 0:E], float(CAP), None, ALU.min))
            link(V.tensor_scalar(n_room[:, :], n_first[:, :], -1.0, float(CAP), ALU.mult, ALU.add))
            link(V.tensor_tensor(n_second[:, :], last_carry[:, E:2 * E], n_room[:, :], ALU.min))
            link(V.tensor_tensor(n_kept[:, :], n_first[:, :], n_second[:, :], ALU.add))
            link(V.tensor_scalar(nt_i[:, :], n_kept[:, :], float(P - 1), None, ALU.add))
            link(V.tensor_scalar(nt_sh[:, :], nt_i[:, :], 7, None, ALU.logical_shift_right))
            link(V.tensor_copy(nt_f[:, :], nt_sh[:, :]))
            link(V.tensor_tensor(t_mul[:, :, :], earlier[:, :, :], nt_f[:, :].unsqueeze(1).to_broadcast([1, E, E]), ALU.mult))
            link(V.tensor_reduce(t_first[:, :], t_mul[:, :, :], AX.X, ALU.add))
            link(V.tensor_tensor(t_end[:, :], t_first[:, :], nt_f[:, :], ALU.add))
            link(V.tensor_tensor(r_start[:, :], region_i[:, :], n_second[:, :], ALU.subtract))
            link(V.tensor_tensor(pad_tab[:, :], r_start[:, :], n_kept[:, :], ALU.add))
            link(V.scalar_tensor_tensor(out=r_off[:, :], in0=t_first[:, :], scalar=float(-P), in1=r_start[:, :], op0=ALU.mult, op1=ALU.add))
            link(V.tensor_tensor(r_step[:, 0:E - 1], r_off[:, 1:E], r_off[:, 0:E - 1], ALU.subtract))
            link(V.tensor_tensor(past[:, :, :], tile_i[:, :].unsqueeze(2).to_broadcast([1, NT, E]),
                                 t_end[:, :].unsqueeze(1).to_broadcast([1, NT, E]), ALU.is_ge))
            link(V.tensor_reduce(tile_e[:, :], past[:, :, 0:E - 1], AX.X, ALU.add))
            link(V.tensor_copy(expert_tab[:, :], tile_e[:, :]))
            link(V.tensor_tensor(past_step[:, :, 0:E - 1], past[:, :, 0:E - 1],
                                 r_step[:, 0:E - 1].unsqueeze(1).to_broadcast([1, NT, E - 1]), ALU.mult))
            link(V.tensor_reduce(tile_r[:, :], past_step[:, :, 0:E - 1], AX.X, ALU.add))
            link(V.scalar_tensor_tensor(out=tile_r2[:, :], in0=tile_i[:, :], scalar=float(P), in1=tile_r[:, :], op0=ALU.mult, op1=ALU.add))
            link(V.tensor_scalar(tile_r3[:, :], tile_r2[:, :], r_off[:, 0:1], float(-PAD_ROW), ALU.add, ALU.add))
            link(V.tensor_scalar(tile_r[:, :], past[:, :, E - 1], -1.0, 1.0, ALU.mult, ALU.add))
            link(V.tensor_tensor(tile_r4[:, :], tile_r3[:, :], tile_r[:, :], ALU.mult))
            V.tensor_scalar(row_tab[:, :], tile_r4[:, :], float(PAD_ROW), None, ALU.add).then_inc(table_done, 1)

            V.tensor_tensor(tdiff[:, :, :], top_all[:, :, :], top_all[:, :, 0:1].to_broadcast([P, B, 8]), ALU.subtract).then_inc(gexp_ready, 1)
            dve.wait_ge(gexp_done, 1)
            link(V.tensor_reduce(gsum[:, :], texp[:, :, :], AX.X, ALU.add))
            link(V.tensor_scalar(gden[:, :], gsum[:, :], GATE_EPS, 1.0, ALU.mult, ALU.add))
            link(V.tensor_tensor(gden2[:, :], gden[:, :], texp[:, :, 1], ALU.add))
            link(V.reciprocal(grec[:, :], gden2[:, :]))
            link(V.tensor_scalar(gw[:, 0, :], grec[:, :], tanh_g[:, 1:2], None, ALU.mult))
            link(V.tensor_tensor(gw[:, 1, :], gw[:, 0, :], texp[:, :, 1], ALU.mult))

            dve.wait_ge(moe_loaded, 48)

            def early(i, v):
                t = i * 4 + v
                e = dve.value_load(expert_tab[0:1, bass.ds(t, 1)], min_val=0, max_val=E - 1)
                wait(dve, y_ready[v], i)
                wait(dve, hT_ready, t - 3)
                V.tensor_copy(ex_cur[:, v, :], ex_sb[:, bass.ds(e, 1), :].rearrange("p e f -> p (e f)")).then_inc(ex_ready, 1)
                wait(dve, xt_loaded[v], i * 16 + 16)
                wait(dve, y_out[v], i * 16)
                V.tensor_copy(dest[:, v, :], xt[:, v, D:D + 1].bitcast(U32)).then_inc(dest_ready, 1)
                dve.wait_ge(xt_psum, t + 1)
                V.tensor_copy(xtT[:, v % 2, :], X_BANK[v % 2][:, 0:P]).then_inc(xtT_ready, 1)

            def back(i, v):
                t = i * 4 + v
                dve.wait_ge(y_psum, t + 1)
                V.tensor_tensor(y_s[:, v, :], Y_BANK[v % 2][:, 0:D], ex_cur[:, v, FF:FF + D], ALU.add).then_inc(y_ready[v], 1)

            tiles(dve, early, lambda i, v: None, back)

            for k in range(NC):
                dve.wait_ge(yc_loaded[k], 16 * K)
                for s in range(CH * k, CH * k + CH):
                    xv = x_all[:, s * D:s * D + D]
                    V.scalar_tensor_tensor(out=xv, in0=yc[:, 0, s, :], scalar=gw[:, 0, s:s + 1], in1=xv, op0=ALU.mult, op1=ALU.add).then_inc(fin_step, 1)
                    dve.wait_ge(fin_step, s + 1)
                    V.scalar_tensor_tensor(out=xv, in0=yc[:, 1, s, :], scalar=gw[:, 1, s:s + 1], in1=xv, op0=ALU.mult, op1=ALU.add).then_inc(fin_done, 1)


_INS = ['x', 'ctx_1024', 'g_xattn', 'g_ffn', 'L0_xattn_w_out', 'L0_xattn_b_out', 'L0_ffn_Wg', 'L0_ffn_W1', 'L0_ffn_b1',
        'L0_ffn_W2', 'L0_ffn_b2']


def kernel(**inputs):
    import numpy as _np
    import concourse.bacc as _bacc
    from concourse import mybir as _mybir
    from concourse.bass_utils import run_bass_kernel_spmd as _run

    nc = _bacc.Bacc("TRN2", target_bir_lowering=False, num_devices=1)
    arrays, args = {}, []
    for name in _INS:
        a = _np.ascontiguousarray(inputs[name])
        arrays[f"in_{name}_dram"] = a
        args.append(nc.dram_tensor(f"in_{name}_dram", a.shape, _mybir.dt.from_np(a.dtype), kind="ExternalInput").ap())
    shape = inputs["x"].shape
    args.append(nc.dram_tensor("out_0_dram", shape, _mybir.dt.float32, kind="ExternalOutput").ap())
    flamingo_layer(nc, *args)
    r = _run(nc, [arrays], core_ids=[0])
    return r.results[0]["out_0_dram"]
```

```python
from collections import namedtuple
from contextlib import ExitStack

import concourse.bass as bass
from concourse import mybir

F32 = mybir.dt.float32
BF16 = mybir.dt.bfloat16
I32 = mybir.dt.int32
U32 = mybir.dt.uint32
ALU = mybir.AluOpType
ACT = mybir.ActivationFunctionType
AX = mybir.AxisListType

P = 128
HD = 8
LN_EPS = 1e-5
GATE_EPS = 1e-9

TERMS = (("low", "high"), ("middle", "high"), ("high", "high"), ("high", "middle"), ("high", "low"), ("middle", "middle"))

class Seq(namedtuple("Seq", "quad place")):

    @property
    def is_first(self):
        return isinstance(self.quad, int) and self.quad == 0 and self.place == 0

    @property
    def slot(self):
        return self.place % 2

    @property
    def pair(self):
        return self.quad * 2 + self.place // 2


def flamingo_layer(nc, x, ctx, g_xattn, g_ffn, w_out, b_out, Wg, W1, b1, W2, b2, out):
    B, S, D = x.shape
    E = Wg.shape[1]
    FF = W1.shape[2]
    T = B * S
    K = 2
    CAP = 2 * K * T // E
    H = D // HD
    G = 4
    J = H // G
    KS = len(TERMS) * HD
    SCALE = 1.0 / float(D) ** 0.5
    NF = FF // P
    MID = T
    REGION = 2 * T + P
    PAD_ROW = E * REGION
    NT = 72
    assert NT % 4 == 0 and NT * P > K * T + (E - 1) * (P - 1) and S == P and D == P
    ROW = D + 1
    CH = 4
    NC = B // CH

    xs_dram = nc.dram_tensor("expert_rows", [PAD_ROW + P, ROW], F32, kind="Internal").ap()
    y_dram = nc.dram_tensor("choice_rows", [K * T, D], F32, kind="Internal").ap()

    with ExitStack() as es:
        def sb(name, shape, dt=F32):
            return es.enter_context(nc.sbuf_tensor(name, shape, dt))

        def sem(name):
            return es.enter_context(nc.semaphore(name))

        bank = [es.enter_context(nc.psum_tensor(f"bank{i}", [P, 512], F32)) for i in range(8)]

        col_i = sb("col_i", [P, P], I32)
        diff_i = sb("diff_i", [P, P], I32)
        ident = sb("ident", [P, P])
        ident_b = sb("ident_b", [P, P], BF16)
        before = sb("before", [P, P], BF16)
        ones_b = sb("ones_b", [P, P], BF16)
        neg_half = sb("neg_half", [P, 1])
        iota8 = sb("iota8", [P, 8])
        ids = sb("ids", [P, B, 2], I32)
        pos_sign = sb("pos_sign", [P, 2])
        pos_base = sb("pos_base", [P, 2])
        zeros = sb("zeros", [P, 1024])
        pad = sb("pad", [P, ROW])
        wout_sb = sb("wout_sb", [P, D])
        wout_p = sb("wout_p", [P, D])
        woutT = sb("woutT", [P, D])
        bias_out = sb("bias_out", [P, D])
        gates = sb("gates", [P, 2])
        tanh_g = sb("tanh_g", [P, 2])
        wg_sb = sb("wg_sb", [P, E])
        ED = FF + D + NF
        ex_sb = sb("ex_sb", [P, E, ED])
        w2_sb = sb("w2_sb", [P, E * NF * D])
        b1_rows = sb("b1_rows", [E * NF, P])
        x_all = sb("x_all", [P, B * D])
        ctx_all = sb("ctx_all", [P, B * D])
        st1 = sb("st1", [P, 2, 6])
        mv1 = sb("mv1", [P, 2, 2])
        ve1 = sb("ve1", [P, 2])
        rstd1 = sb("rstd1", [P, 2])
        st2 = sb("st2", [P, 2, 6])
        mv2 = sb("mv2", [P, 2, 2])
        ve2 = sb("ve2", [P, 2])
        rstd2 = sb("rstd2", [P, 2])
        xn = sb("xn", [P, 2, D])
        ctx_d = sb("ctx_d", [P, 2, D])
        parts = sb("parts", [P, 2, 2 * len(TERMS), P], BF16)
        rest = sb("rest", [P, 2, 2, P])
        stack = sb("stack", [P, 4, H, 2 * P], BF16)
        values = sb("values", [P, 2, 2, 2, G, 32])
        negmax = sb("negmax", [P, 2, H], BF16)
        mT = sb("mT", [H, 2, P], BF16)
        probs = sb("probs", [P, 2, G, J * P])
        oS = sb("oS", [P, 2, 2 * P])
        rsum = sb("rsum", [P, 2, H])
        attn = sb("attn", [P, 2, D])
        aT = sb("aT", [P, 2, P])
        xrow = sb("xrow", [P, 4, 2, ROW])
        xn2T = sb("xn2T", [P, 2, P])
        lg = sb("lg", [P, 2, E])
        top = sb("top", [P, 2, 8])
        topi = sb("topi", [P, 2, 8], U32)
        idxf = sb("idxf", [P, 2, 2])
        chosen = sb("chosen", [P, 2, 2, E], BF16)
        carry = sb("carry", [P, 2, 2 * E])
        place = sb("place", [P, 2, E])
        place2 = sb("place2", [P, 2, E])
        pos = sb("pos", [P, 2])
        pos2 = sb("pos2", [P, 2])
        pos3 = sb("pos3", [P, 2])
        slot_i = sb("slot_i", [P, 4, 2], U32)
        top_all = sb("top_all", [P, B, 8])
        tdiff = sb("tdiff", [P, B, 8])
        texp = sb("texp", [P, B, 8])
        gsum = sb("gsum", [P, B])
        gden = sb("gden", [P, B])
        gden2 = sb("gden2", [P, B])
        gw = sb("gw", [P, 2, B])
        grec = sb("grec", [P, B])
        n_first = sb("n_first", [1, E])
        n_room = sb("n_room", [1, E])
        n_second = sb("n_second", [1, E])
        n_kept = sb("n_kept", [1, E])
        nt_i = sb("nt_i", [1, E], I32)
        nt_sh = sb("nt_sh", [1, E], I32)
        nt_f = sb("nt_f", [1, E])
        pair_i = sb("pair_i", [1, E, E], I32)
        earlier = sb("earlier", [1, E, E])
        t_mul = sb("t_mul", [1, E, E])
        t_first = sb("t_first", [1, E])
        t_end = sb("t_end", [1, E])
        region_i = sb("region_i", [1, E])
        r_start = sb("r_start", [1, E])
        r_off = sb("r_off", [1, E])
        r_step = sb("r_step", [1, E])
        tile_i = sb("tile_i", [1, NT])
        past = sb("past", [1, NT, E])
        past_step = sb("past_step", [1, NT, E])
        tile_e = sb("tile_e", [1, NT])
        tile_r = sb("tile_r", [1, NT])
        tile_r2 = sb("tile_r2", [1, NT])
        tile_r3 = sb("tile_r3", [1, NT])
        tile_r4 = sb("tile_r4", [1, NT])
        expert_tab = sb("expert_tab", [1, NT], I32)
        row_tab = sb("row_tab", [1, NT], I32)
        pad_tab = sb("pad_tab", [1, E], I32)
        xt = sb("xt", [P, 4, ROW])
        dest = sb("dest", [P, 4, 1], U32)
        xtT = sb("xtT", [P, 2, P])
        ex_cur = sb("ex_cur", [P, 4, ED])
        hT = sb("hT", [P, 2, NF, P])
        y_s = sb("y_s", [P, 4, D])
        yc = stack[:, :, :, :].rearrange("p s h q -> p (s h q)").bitcast(F32).rearrange("p (k b d) -> p k b d", k=K, b=B)

        S_BANK, E_BANK = bank[0:2], bank[2:4]
        TA, TB, O_BANK, R_BANK = bank[4], bank[5], bank[6], bank[7]
        PROJ, A_T = O_BANK[:, 256:256 + D], O_BANK[:, 384:384 + P]
        O_T = TA[:, 2 * P:4 * P].rearrange("p (x k) -> p x k", k=16)
        TB_max = TB[0:H, 256:256 + P // 2].bitcast(BF16)
        X_BANK, H_BANK, Y_BANK = bank[0:2], bank[2:4], bank[4:6]

        iota_done, const_done, chain = sem("iota_done"), sem("const_done"), sem("chain")
        pool_const = sem("pool_const")
        gate_loaded, w_loaded, x_loaded, moe_loaded = sem("gate_loaded"), sem("w_loaded"), sem("x_loaded"), sem("moe_loaded")
        wout_ordered = sem("wout_ordered")
        tanh_done, woutT_psum, b1T_psum, prep_done = sem("tanh_done"), sem("woutT_psum"), sem("b1T_psum"), sem("prep_done")
        zeroed = sem("zeroed")
        ctx_loaded = sem("ctx_loaded")
        ctx_d_ready = sem("ctx_d_ready")
        stack_free = sem("stack_free")
        stack_in = [sem(f"stack_in{u}") for u in range(2)]
        mT_in = [sem(f"mT_in{u}") for u in range(2)]
        ln1_stats, ln1_aggr, ln1_var, ln1_rstd, xn_ready = sem("ln1_stats"), sem("ln1_aggr"), sem("ln1_var"), sem("ln1_rstd"), sem("xn_ready")
        xb_done = sem("xb_done")
        qkT_ready, high_ready, rest_ready = sem("qkT_ready"), sem("high_ready"), sem("rest_ready")
        middle_ready, parts_ready, values_ready = sem("middle_ready"), sem("parts_ready"), sem("values_ready")
        oS_ready, oT_psum, attn_ready, attnT_psum = sem("oS_ready"), sem("oT_psum"), sem("attn_ready"), sem("attnT_psum")
        s_ready, max_done, m_psum, mT_ready = sem("s_ready"), sem("max_done"), sem("m_psum"), sem("mT_ready")
        e_ready, exp_done, o_ready = sem("e_ready"), sem("exp_done"), sem("o_ready")
        rsum_done, aT_ready, proj_ready = sem("rsum_done"), sem("aT_ready"), sem("proj_ready")
        x1_done, ln2_stats, ln2_aggr, ln2_var, ln2_rstd = sem("x1_done"), sem("ln2_stats"), sem("ln2_aggr"), sem("ln2_var"), sem("ln2_rstd")
        xn2_ready, xn2T_psum, xn2T_ready = sem("xn2_ready"), sem("xn2T_psum"), sem("xn2T_ready")
        logit_ready, lg_done, chosen_done = sem("logit_ready"), sem("lg_done"), sem("chosen_done")
        top_max, top_idx, top_num = sem("top_max"), sem("top_idx"), sem("top_num")
        cum_ready, slot_done = sem("cum_ready"), sem("slot_done")
        place_done, carry_done, picked, pos_summed, pos_signed, pos_based = [
            sem(s) for s in ("place_done", "carry_done", "picked", "pos_summed", "pos_signed", "pos_based")]
        row_out = [sem(f"row_out{u}") for u in range(4)]
        gexp_ready, gexp_done, gw_step = sem("gexp_ready"), sem("gexp_done"), sem("gw_step")
        table_step, table_done, pads_out = sem("table_step"), sem("table_done"), sem("pads_out")
        xt_loaded = [sem(f"xt_loaded{v}") for v in range(4)]
        xt_psum, xtT_ready, ex_ready, dest_ready = sem("xt_psum"), sem("xtT_ready"), sem("ex_ready"), sem("dest_ready")
        h_psum, hT_ready, y_psum = sem("h_psum"), sem("hT_ready"), sem("y_psum")
        y_ready = [sem(f"y_ready{v}") for v in range(4)]
        y_out = [sem(f"y_out{v}") for v in range(4)]
        yc_loaded = [sem(f"yc_loaded{k}") for k in range(NC)]
        fin_step, fin_done = sem("fin_step"), sem("fin_done")
        stored = sem("stored")

        def at(s, scale=1, plus=0):
            return s.quad * (4 * scale) + (s.place * scale + plus)

        def wait(eng, semaphore, value):
            if isinstance(value, int) and value < 1:
                return
            eng.wait_ge(semaphore, value)

        def wait_alone(eng, semaphore, value):
            eng.wait_ge(const_done, 1)
            eng.wait_ge(semaphore, value)

        def cols(s, width=P):
            return bass.ds(at(s, width), width) if not isinstance(s.quad, int) else slice(at(s, width), at(s, width) + width)

        def by_head(columns):
            return columns.rearrange("p (d h) -> p h d", d=HD)

        def pipeline(eng, step):
            BEHIND = (1, 0, -2, -3, -4, -5, -6, -7, -8)

            def due(t):
                return [Seq(k // 4, k % 4) if 0 <= k < B else None for k in (t + k for k in BEHIND)]

            FIRST, LAST = 8, B - 4
            for t in range(-1, FIRST):
                step(*due(t))
            with eng.Fori(FIRST // 4, LAST // 4) as i:
                for u in range(4):
                    step(*[Seq(i + (u + k) // 4, (u + k) % 4) for k in BEHIND])
            for t in range(LAST, B - min(BEHIND)):
                step(*due(t))

        def tiles(eng, early, front, back):
            NI = NT // 4

            def turn(i, v, ahead):
                for part, k in ((early, 2), (front, 1), (back, 0)):
                    if v + k < 4 or ahead:
                        part(i + (v + k) // 4, (v + k) % 4)

            early(0, 0)
            early(0, 1)
            front(0, 0)
            for v in range(4):
                turn(0, v, True)
            with eng.Fori(1, NI - 1) as i:
                for v in range(4):
                    turn(i, v, True)
            for v in range(4):
                turn(NI - 1, v, False)

        block = es.enter_context(nc.Block())

        @block.sync
        def _(sp):
            xv = x.rearrange("b s d -> s b d")
            xa = x_all[:, :].rearrange("p (b d) -> p b d", b=B)
            sp.dma_start(xa[:, 0:2, :], xv[:, 0:2, :]).then_inc(x_loaded, 16)
            cv = ctx.rearrange("b s d -> s b d")
            ca = ctx_all[:, :].rearrange("p (b d) -> p b d", b=B)
            sp.dma_start(ca[:, 0:2, :], cv[:, 0:2, :]).then_inc(ctx_loaded, 16)
            sp.dma_start(gates[:, 0:1], g_xattn.partition_broadcast(P)).then_inc(gate_loaded, 16)
            sp.dma_start(gates[:, 1:2], g_ffn.partition_broadcast(P)).then_inc(gate_loaded, 16)
            sp.dma_start(wout_sb[:, :], w_out).then_inc(w_loaded, 16)
            sp.dma_start(bias_out[:, :], b_out.partition_broadcast(P)).then_inc(w_loaded, 16)
            sp.dma_start(b1_rows[:, :], b1.rearrange("e (c f) -> (e c) f", c=NF)).then_inc(w_loaded, 16)
            sp.dma_start(wg_sb[:, :], Wg).then_inc(w_loaded, 16)
            sp.dma_start(xa[:, 2:8, :], xv[:, 2:8, :]).then_inc(x_loaded, 16)
            sp.dma_start(ca[:, 2:8, :], cv[:, 2:8, :]).then_inc(ctx_loaded, 16)
            sp.dma_start(xa[:, 8:B, :], xv[:, 8:B, :]).then_inc(x_loaded, 16)
            sp.dma_start(ca[:, 8:B, :], cv[:, 8:B, :]).then_inc(ctx_loaded, 16)
            sp.dma_start(ex_sb[:, :, 0:FF], W1.rearrange("e d f -> d e f")).then_inc(moe_loaded, 16)
            sp.dma_start(w2_sb[:, :].rearrange("p (e c d) -> p e c d", e=E, c=NF),
                         W2.rearrange("e (c f) d -> f e c d", c=NF)).then_inc(moe_loaded, 16)
            sp.dma_start(ex_sb[:, :, FF:FF + D], b2.partition_broadcast(P)).then_inc(moe_loaded, 16)
            sp.wait_ge(pool_const, 1)
            zrows = y_dram[0:K * T, :].rearrange("(k p r) d -> k p (r d)", p=P, r=8)
            for k in range(K * T // (8 * P)):
                sp.dma_start(zrows[k], zeros[:, :]).then_inc(zeroed, 16)

            def step(n, a, m, b, p, q, c, r, d):
                if b:
                    sp.wait_ge(mT_ready, at(b, 1, 1))
                    sp.dma_start(stack[KS:KS + 1, b.place, :, 0:P], mT[:, b.slot, :]).then_inc(mT_in[b.slot], 16)
                if a:
                    sp.wait_ge(parts_ready, at(a, 1, 1))
                    sp.wait_ge(stack_free, at(a, 1, 1))
                    for t in range(len(TERMS)):
                        sp.dma_start(stack[HD * t:HD * t + HD, a.place, :, :],
                                     parts[:, a.slot, 2 * t:2 * t + 2, :].rearrange("p b q -> p (b q)")).then_inc(stack_in[a.slot], 16)

            pipeline(sp, step)

            sp.wait_ge(table_done, 1)
            for u in range(4):
                sp.wait_ge(row_out[u], 32 * (B // 4))
            for e in range(E):
                r = sp.value_load(pad_tab[0:1, e:e + 1], min_val=0, max_val=PAD_ROW)
                sp.dma_start(xs_dram[bass.ds(r, P), :], pad[:, :]).then_inc(pads_out, 16)
            sp.dma_start(xs_dram[PAD_ROW:PAD_ROW + P, :], pad[:, :]).then_inc(pads_out, 16)
            sp.wait_ge(pads_out, 16 * (E + 1))

            def load_tile(i, v):
                t = i * 4 + v
                wait(sp, xt_psum, t - 3)
                wait(sp, dest_ready, t - 3)
                r = sp.value_load(row_tab[0:1, bass.ds(t, 1)], min_val=0, max_val=PAD_ROW)
                sp.dma_start(xt[:, v, :], xs_dram[bass.ds(r, P), :]).then_inc(xt_loaded[v], 16)

            for v in range(4):
                load_tile(0, v)
            with sp.Fori(1, NT // 4) as i:
                for v in range(4):
                    load_tile(i, v)

            for v in range(4):
                sp.wait_ge(y_out[v], 16 * (NT // 4))
            yv = y_dram[0:K * T, :].rearrange("(c b p) d -> c p b d", c=K, p=P)
            for k in range(NC):
                for c in range(K):
                    sp.dma_start(yc[:, c, CH * k:CH * k + CH, :], yv[c, :, CH * k:CH * k + CH, :]).then_inc(yc_loaded[k], 16)
            ov = out.rearrange("b s d -> s b d")
            for k in range(NC):
                sp.wait_ge(fin_done, CH * (k + 1))
                sp.dma_start(ov[:, CH * k:CH * k + CH, :], xa[:, CH * k:CH * k + CH, :]).then_inc(stored, 16)
            sp.wait_ge(stored, 16 * NC)

        @block.gpsimd
        def _(pool):
            nc.gpsimd.iota(col_i[:, :], [[1, P]], base=0, channel_multiplier=0)
            nc.gpsimd.iota(diff_i[:, :], [[1, P]], base=0, channel_multiplier=-1)
            nc.gpsimd.iota(ids[:, :, :], [[P, B], [T, 2]], base=0, channel_multiplier=1)
            nc.gpsimd.iota(pair_i[:, :, :], [[-1, E], [1, E]], base=0, channel_multiplier=0)
            nc.gpsimd.iota(region_i[:, :], [[REGION, E]], base=MID, channel_multiplier=0, allow_small_or_imprecise_dtypes=True)
            nc.gpsimd.iota(tile_i[:, :], [[1, NT]], base=0, channel_multiplier=0, allow_small_or_imprecise_dtypes=True)
            nc.gpsimd.iota(pad[:, D:D + 1].bitcast(I32), [[0, 1]], base=K * T, channel_multiplier=1)
            nc.gpsimd.memset(pad[:, 0:D], 0.0)
            nc.gpsimd.memset(ones_b[:, :], 1.0)
            nc.gpsimd.memset(neg_half[:, :], -0.5)
            nc.gpsimd.memset(carry[:, 1, :], 0.0)
            nc.gpsimd.memset(pos_sign[:, 0:1], 1.0)
            nc.gpsimd.memset(pos_sign[:, 1:2], -1.0)
            nc.gpsimd.memset(pos_base[:, 0:1], float(MID))
            nc.gpsimd.memset(pos_base[:, 1:2], float(MID - 1)).then_inc(iota_done, 1)
            nc.gpsimd.memset(stack[:, :, :, P:2 * P], 1.0)
            nc.gpsimd.memset(stack[:, :, :, 0:P], 0.0).then_inc(stack_free, 4)
            for j in range(2):
                nc.gpsimd.memset(values[:, :, :, j, :, 16 * (1 - j):16 * (2 - j)], 0.0)
                nc.gpsimd.memset(values[:, :, :, j, :, 16 * j + HD:16 * j + 16], 1.0)
            nc.gpsimd.memset(zeros[:, :], 0.0).then_inc(pool_const, 1)

            def step(n, a, m, b, p, q, c, r, d):
                if c:
                    pool.wait_ge(ln2_var, at(c, 1, 1))
                    nc.gpsimd.tensor_tensor(rstd2[:, c.slot:c.slot + 1], ve2[:, c.slot:c.slot + 1], neg_half[:, :],
                                            ALU.pow).then_inc(ln2_rstd, 1)
                if n:
                    pool.wait_ge(ln1_var, at(n, 1, 1))
                    nc.gpsimd.tensor_tensor(rstd1[:, n.slot:n.slot + 1], ve1[:, n.slot:n.slot + 1], neg_half[:, :],
                                            ALU.pow).then_inc(ln1_rstd, 1)
                if b:
                    if b.is_first:
                        pool.wait_ge(pool_const, 1)
                        pool.wait_ge(ctx_loaded, 16 * 3)
                    wait(pool, o_ready, at(b, 1, -1))
                    by_strip = ctx_all[:, cols(b)].rearrange("p (g s j d) -> p s g j d", g=G, s=2, j=2)
                    for j in range(2):
                        last = nc.gpsimd.tensor_copy(values[:, b.slot, :, j, :, 16 * j:16 * j + HD], by_strip[:, :, :, j, :])
                    last.then_inc(values_ready, 1)
                if a:
                    if a.is_first:
                        pool.wait_ge(prep_done, 3)
                    pool.wait_ge(xn_ready, at(a, 1, 1))
                    if d:
                        pool.wait_ge(slot_done, at(d, 1, 1))
                    nc.gpsimd.tensor_tensor(x_all[:, cols(a)], x_all[:, cols(a)], bias_out[:, :], ALU.add).then_inc(xb_done, 1)
                if d:
                    if not a:
                        pool.wait_ge(slot_done, at(d, 1, 1))
                    for k in range(2):
                        nc.gpsimd.indirect_dma_start(
                            xs_dram, bass.IndirectOffsetOnAxis(ap=slot_i[:, d.place, k:k + 1], axis=0),
                            xrow[:, d.place, k, :], None).then_inc(row_out[d.place], 16)

            pipeline(pool, step)

            pool.wait_ge(zeroed, 16 * (K * T // (8 * P)))

            last_row = pool.snap(K * T - 1)
            with pool.Fori(1, NT // 4 + 1) as i:
                for v in range(4):
                    wait_alone(pool, y_ready[v], i)
                    nc.gpsimd.indirect_dma_start(y_dram, bass.IndirectOffsetOnAxis(ap=dest[:, v, :], axis=0), y_s[:, v, :],
                                                 None, bounds_check=last_row, oob_is_err=False).then_inc(y_out[v], 16)

        @block.scalar
        def _(act):
            act.wait_ge(gate_loaded, 32)
            nc.scalar.activation(tanh_g[:, :], gates[:, :], ACT.Tanh).then_inc(tanh_done, 1)

            def step(n, a, m, b, p, q, c, r, d):
                if c:
                    act.wait_ge(attnT_psum, at(c, 1, 1))
                    wait(act, proj_ready, at(c, 1, -1))
                    nc.scalar.copy(aT[:, c.slot, :], A_T).then_inc(aT_ready, 1)
                if b:
                    act.wait_ge(m_psum, at(b, 1, 1))
                    wait(act, mT_in[b.slot], b.pair * 16)
                    nc.scalar.copy(mT[:, b.slot, :], TB_max).then_inc(mT_ready, 1)
                if n:
                    if n.is_first:
                        act.wait_ge(ctx_loaded, 16 * 3)
                    wait(act, qkT_ready, at(n, 1, -1))
                    nc.scalar.copy(by_head(ctx_d[:, n.slot, :]), ctx_all[:, cols(n)].rearrange("p (h d) -> p h d", d=HD)).then_inc(ctx_d_ready, 1)
                if r:
                    act.wait_ge(xn2T_psum, at(r, 1, 1))
                    wait(act, logit_ready, at(r, 1, -1))
                    nc.scalar.copy(xn2T[:, r.slot, :], TB[:, P:2 * P]).then_inc(xn2T_ready, 1)
                if a:
                    act.wait_ge(qkT_ready, at(a, 1, 1))
                    wait(act, stack_in[a.slot], a.pair * (16 * len(TERMS)))
                    for o, blocks in ((0, slice(4, 9, 2)), (P, slice(1, 6, 2))):
                        last = nc.scalar.copy(parts[:, a.slot, blocks, :], TA[:, o:o + P].unsqueeze(1).to_broadcast([P, 3, P]))
                    last.then_inc(high_ready, 1)

                    act.wait_ge(rest_ready, at(a, 1, 1))
                    for o, blocks in ((0, slice(2, 11, 8)), (1, slice(7, 12, 4))):
                        last = nc.scalar.copy(parts[:, a.slot, blocks, :], rest[:, a.slot, o:o + 1, :].to_broadcast([P, 2, P]))
                    last.then_inc(middle_ready, 1)
                def exp(g):
                    if b:
                        act.wait_ge(e_ready, at(b, G, g + 1))
                        if g == 0:
                            wait(act, o_ready, at(b, 1, -1))
                        nc.scalar.activation(probs[:, b.slot, g, :], E_BANK[g % 2][:, :], ACT.Exp,
                                             scale=SCALE).then_inc(exp_done, 1)

                exp(0)
                exp(1)
                exp(2)
                if p:
                    act.wait_ge(o_ready, at(p, 1, 1))
                    wait(act, oT_psum, at(p, 1, -1))
                    nc.scalar.copy(oS[:, p.slot, :], O_BANK[:, 0:2 * P]).then_inc(oS_ready, 1)
                exp(3)

            pipeline(act, step)

            act.wait_ge(gexp_ready, 1)
            nc.scalar.activation(texp[:, :, :], tdiff[:, :, :], ACT.Exp).then_inc(gexp_done, 1)

            def gelu(i, v):
                t = i * 4 + v
                act.wait_ge(h_psum, t + 1)
                wait(act, y_psum, t - 1)
                for c in range(NF):
                    last = nc.scalar.activation(hT[:, v % 2, c, :], H_BANK[v % 2][:, c * P:c * P + P], ACT.Gelu,
                                                bias=ex_cur[:, v, FF + D + c:FF + D + c + 1])
                last.then_inc(hT_ready, 1)

            for v in range(4):
                gelu(0, v)
            with act.Fori(1, NT // 4) as i:
                for v in range(4):
                    gelu(i, v)

        @block.tensor
        def _(pe):
            pe.wait_ge(const_done, 1)
            pe.wait_ge(w_loaded, 64)
            pe.wait_ge(wout_ordered, 1)
            nc.tensor.transpose(TA[:, 0:P], wout_p[:, :], ident[:, :]).then_inc(woutT_psum, 1)
            nc.tensor.transpose(TB[:, 0:E * NF], b1_rows[:, :], ident[0:E * NF, 0:E * NF]).then_inc(b1T_psum, 1)
            pe.wait_ge(prep_done, 3)

            def step(n, a, m, b, p, q, c, r, d):
                def main_scores(g):
                    if not b:
                        return
                    if g == 0:
                        pe.wait_ge(mT_in[b.slot], b.pair * 16 + 16)
                    wait(pe, exp_done, at(b, G, g - 1))
                    for j in range(J):
                        head = stack[:, b.place, J * g + j, :]
                        last = nc.tensor.matmul(E_BANK[g % 2][:, j * P:j * P + P], head[:, P:2 * P], head[:, 0:P],
                                                start=True, stop=True)
                    last.then_inc(e_ready, 1)

                def max_scores(g):
                    if not m:
                        return
                    if g == 0:
                        pe.wait_ge(stack_in[m.slot], (m.pair + 1) * (16 * len(TERMS)))
                    wait(pe, max_done, at(m, G, g - 1))
                    for j in range(J):
                        head = stack[0:KS, m.place, J * g + j, :]
                        last = nc.tensor.matmul(S_BANK[g % 2][:, j * P:j * P + P], head[:, 0:P], head[:, P:2 * P],
                                                start=True, stop=True)
                        if b and g == 3 and j == 0:
                            last.then_inc(stack_free, 1)
                    last.then_inc(s_ready, 1)

                def sums(h2):
                    if not p:
                        return
                    if h2 == 0:
                        pe.wait_ge(exp_done, at(p, G, G))
                        pe.wait_ge(values_ready, at(p, 1, 1))
                        if c:
                            pe.wait_ge(x1_done, at(c, 1, 1))
                        wait(pe, oS_ready, at(p))
                    for j in range(2):
                        head = (2 * h2 + j) * P
                        for g in range(G):
                            last = nc.tensor.matmul(O_BANK[32 * g:32 * g + 32, h2 * P:h2 * P + P], values[:, p.slot, h2, j, g, :],
                                                    probs[:, p.slot, g, head:head + P],
                                                    start=(j == 0), stop=(j == 1), skip_group_check=True)
                    if h2 == 1:
                        last.then_inc(o_ready, 1)

                if c:
                    pe.wait_ge(attn_ready, at(c, 1, 1))
                    pe.wait_ge(oS_ready, at(q, 1, 1) if q else B)
                    nc.tensor.transpose(A_T, attn[:, c.slot, :], ident[:, :]).then_inc(attnT_psum, 1)
                if b:
                    pe.wait_ge(max_done, at(b, G, G))
                    wait(pe, xn2T_ready, at(r) if r else 0)
                    nc.tensor.transpose(TB_max, negmax[:, b.slot, :], ident_b[:, :]).then_inc(m_psum, 1)
                if a:
                    pe.wait_ge(ctx_d_ready, at(a, 1, 1))
                    pe.wait_ge(xn_ready, at(a, 1, 1))
                    wait(pe, rest_ready, at(a))
                    if q:
                        wait(pe, attn_ready, at(q))
                    nc.tensor.transpose(TA[:, 0:P], xn[:, a.slot, :], ident[:, :])
                    nc.tensor.transpose(TA[:, P:2 * P], ctx_d[:, a.slot, :], ident[:, :]).then_inc(qkT_ready, 1)
                max_scores(0)
                if r:
                    pe.wait_ge(xn2_ready, at(r, 1, 1))
                    wait(pe, mT_ready, at(b, 1, 1) if b else B)
                    nc.tensor.transpose(TB[:, P:2 * P], xrow[:, r.place, 0, 0:D], ident[:, :]).then_inc(xn2T_psum, 1)
                if c:
                    pe.wait_ge(aT_ready, at(c, 1, 1))
                    nc.tensor.matmul(PROJ, aT[:, c.slot, :], woutT[:, :], start=True, stop=True).then_inc(proj_ready, 1)
                max_scores(1)
                if r:
                    pe.wait_ge(xn2T_ready, at(r, 1, 1))
                    wait(pe, slot_done, at(r))
                    nc.tensor.matmul(R_BANK[:, 0:E], xn2T[:, r.slot, :], wg_sb[:, :], start=True, stop=True).then_inc(logit_ready, 1)
                if q:
                    pe.wait_ge(oS_ready, at(q, 1, 1))
                    wait(pe, rest_ready, at(a, 1, 1) if a else B)
                    wait(pe, attn_ready, at(q))
                    for h2 in range(2):
                        last = nc.tensor.transpose(TA[:, (2 + h2) * P:(3 + h2) * P], oS[:, q.slot, h2 * P:h2 * P + P], ident[:, :])
                    last.then_inc(oT_psum, 1)
                sums(0)
                main_scores(0)
                main_scores(1)
                max_scores(2)
                main_scores(2)
                sums(1)
                main_scores(3)
                max_scores(3)
                if r:
                    pe.wait_ge(chosen_done, at(r, 1, 1))
                    pe.wait_ge(lg_done, at(r, 1, 1))
                    pick = chosen[:, r.slot, :, :].rearrange("p k e -> p (k e)")
                    nc.tensor.matmul(R_BANK[:, 64:64 + 2 * E], before[:, :], pick, start=True, stop=True)
                    nc.tensor.matmul(R_BANK[:, 96:96 + 2 * E], ones_b[:, :], pick, start=True, stop=True).then_inc(cum_ready, 1)

            pipeline(pe, step)

            pe.wait_ge(table_done, 1)
            pe.wait_ge(moe_loaded, 48)

            def early(i, v):
                t = i * 4 + v
                pe.wait_ge(xt_loaded[v], i * 16 + 16)
                wait(pe, xtT_ready, t - 1)
                nc.tensor.transpose(X_BANK[v % 2][:, 0:P], xt[:, v, 0:D], ident[:, :]).then_inc(xt_psum, 1)

            def front(i, v):
                t = i * 4 + v
                pe.wait_ge(xtT_ready, t + 1)
                pe.wait_ge(ex_ready, t + 1)
                wait(pe, hT_ready, t - 1)
                for c in range(NF):
                    last = nc.tensor.matmul(H_BANK[v % 2][:, c * P:c * P + P], ex_cur[:, v, c * P:c * P + P],
                                            xtT[:, v % 2, :], start=True, stop=True)
                last.then_inc(h_psum, 1)

            def back(i, v):
                t = i * 4 + v
                e = pe.value_load(expert_tab[0:1, bass.ds(t, 1)], min_val=0, max_val=E - 1)
                pe.wait_ge(hT_ready, t + 1)
                if v >= 2:
                    pe.wait_ge(y_ready[v - 2], i + 1)
                else:
                    wait(pe, y_ready[v + 2], i)
                for c in range(NF):
                    last = nc.tensor.matmul(Y_BANK[v % 2][:, 0:D], hT[:, v % 2, c, :],
                                            w2_sb[:, bass.ds(e * (NF * D) + c * D, D)], start=(c == 0), stop=(c == NF - 1))
                last.then_inc(y_psum, 1)

            tiles(pe, early, front, back)

        @block.vector
        def _(dve):
            links = [0]

            def link(ins):
                links[0] += 1
                ins.then_inc(chain, 1)
                dve.wait_ge(chain, links[0])

            dve.wait_ge(iota_done, 1)
            V = nc.vector
            V.tensor_scalar(ident[:, :], diff_i[:, :], 0.0, None, ALU.is_equal)
            V.tensor_scalar(ident_b[:, :], diff_i[:, :], 0.0, None, ALU.is_equal)
            V.tensor_scalar(before[:, :], diff_i[:, :], 0.0, None, ALU.is_gt)
            V.tensor_copy(iota8[:, :], col_i[:, 0:8])
            V.tensor_scalar(earlier[:, :, :], pair_i[:, :, :], 0.0, None, ALU.is_lt).then_inc(const_done, 1)
            dve.wait_ge(const_done, 1)
            dve.wait_ge(tanh_done, 1)
            dve.wait_ge(w_loaded, 64)
            V.tensor_copy(wout_p[:, :].rearrange("p (s g k) -> p s g k", s=2, g=G),
                          wout_sb[:, :].rearrange("p (g s k) -> p s g k", s=2, g=G)).then_inc(wout_ordered, 1)
            dve.wait_ge(woutT_psum, 1)
            V.tensor_scalar(woutT[:, :], TA[:, 0:P], tanh_g[:, 0:1], None, ALU.mult).then_inc(prep_done, 1)
            V.tensor_scalar(bias_out[:, :], bias_out[:, :], tanh_g[:, 0:1], None, ALU.mult).then_inc(prep_done, 1)
            dve.wait_ge(b1T_psum, 1)
            V.tensor_copy(ex_sb[:, :, FF + D:ED], TB[:, 0:E * NF].rearrange("p (e c) -> p e c", e=E)).then_inc(prep_done, 1)

            def ln_aggr(mv, st, ve, u, aggr_sem, count, var_sem):
                V.bn_aggr(mv[:, u, :], st[:, u, :]).then_inc(aggr_sem, 1)
                dve.wait_ge(aggr_sem, count)
                V.tensor_scalar(ve[:, u:u + 1], mv[:, u, 1:2], LN_EPS, None, ALU.add).then_inc(var_sem, 1)

            def step(n, a, m, b, p, q, c, r, d):
                def maximum(g):
                    if m:
                        dve.wait_ge(s_ready, at(m, G, g + 1))
                        if g == 0:
                            wait(dve, m_psum, at(m, 1, -1))
                        V.tensor_reduce(negmax[:, m.slot, J * g:J * g + J], S_BANK[g % 2][:, :].rearrange("p (j k) -> p j k", j=J),
                                        AX.X, ALU.max, negate=True).then_inc(max_done, 1)

                maximum(0)
                if c:
                    u = c.slot
                    dve.wait_ge(proj_ready, at(c, 1, 1))
                    dve.wait_ge(xb_done, at(c, 1, 1))
                    V.tensor_tensor(x_all[:, cols(c)], PROJ, x_all[:, cols(c)], ALU.add).then_inc(x1_done, 1)
                if a:
                    u = a.slot
                    dve.wait_ge(high_ready, at(a, 1, 1))
                    wait(dve, parts_ready, at(a, 1, -1))
                    if c:
                        dve.wait_ge(x1_done, at(c, 1, 1))
                    V.tensor_tensor(rest[:, u, :, :], TA[:, 0:2 * P].rearrange("p (o q) -> p o q", o=2), parts[:, u, 4:6, :],
                                    ALU.subtract).then_inc(rest_ready, 1)
                if c:
                    if not a:
                        dve.wait_ge(x1_done, at(c, 1, 1))
                    V.bn_stats(st2[:, c.slot, :], x_all[:, cols(c)]).then_inc(ln2_stats, 1)
                if n:
                    if n.is_first:
                        dve.wait_ge(x_loaded, 16 * 3)
                    V.bn_stats(st1[:, n.slot, :], x_all[:, cols(n)]).then_inc(ln1_stats, 1)
                if c:
                    wait_alone(dve, ln2_stats, at(c, 1, 1))
                    ln_aggr(mv2, st2, ve2, c.slot, ln2_aggr, at(c, 1, 1), ln2_var)
                maximum(1)
                if r:
                    u = r.slot
                    dve.wait_ge(logit_ready, at(r, 1, 1))
                    if n:
                        dve.wait_ge(ln1_stats, at(n, 1, 1))
                    V.tensor_copy(lg[:, u, :], R_BANK[:, 0:E]).then_inc(lg_done, 1)
                if n:
                    if not r:
                        dve.wait_ge(ln1_stats, at(n, 1, 1))
                    ln_aggr(mv1, st1, ve1, n.slot, ln1_aggr, at(n, 1, 1), ln1_var)
                if r:
                    u = r.slot
                    wait_alone(dve, lg_done, at(r, 1, 1))
                    V.max(top[:, u, :], lg[:, u, :]).then_inc(top_max, 1)
                if a:
                    dve.wait_ge(middle_ready, at(a, 1, 1))
                    V.tensor_tensor(parts[:, a.slot, 0:10:9, :], rest[:, a.slot, :, :], parts[:, a.slot, 10:12, :],
                                    ALU.subtract).then_inc(parts_ready, 1)
                if r:
                    wait_alone(dve, top_max, at(r, 1, 1))
                    V.max_index(topi[:, u, :], top[:, u, :], lg[:, u, :]).then_inc(top_idx, 1)
                    V.tensor_copy(top_all[:, bass.ds(at(r), 1), :], top[:, u, :].unsqueeze(1))
                if q:
                    dve.wait_ge(oT_psum, at(q, 1, 1))
                    V.reciprocal(rsum[:, q.slot, :], O_T[:, :, HD]).then_inc(rsum_done, 1)
                if r:
                    dve.wait_ge(top_idx, at(r, 1, 1))
                    V.tensor_copy(idxf[:, u, :], topi[:, u, 0:2]).then_inc(top_num, 1)
                if q:
                    dve.wait_ge(rsum_done, at(q, 1, 1))
                    wait(dve, attnT_psum, at(q, 1, -1))
                    V.tensor_tensor(attn[:, q.slot, :].rearrange("p (x k) -> p x k", k=HD), O_T[:, :, 0:HD],
                                    rsum[:, q.slot, :].unsqueeze(2).to_broadcast([P, H, HD]), ALU.mult).then_inc(attn_ready, 1)
                if r:
                    u = r.slot
                    dve.wait_ge(top_num, at(r, 1, 1))
                    V.tensor_tensor(chosen[:, u, :, :], iota8[:, :].unsqueeze(1).to_broadcast([P, 2, E]),
                                    idxf[:, u, :].unsqueeze(2).to_broadcast([P, 2, E]), ALU.is_equal).then_inc(chosen_done, 1)
                if c:
                    wait(dve, row_out[c.place], c.quad * 32)
                    V.tensor_copy(xrow[:, c.place, :, D:D + 1].bitcast(I32), ids[:, bass.ds(at(c), 1), :].rearrange("p b k -> p (b k)").unsqueeze(2))
                    dve.wait_ge(ln2_rstd, at(c, 1, 1))
                    V.tensor_scalar(xrow[:, c.place, :, 0:D], x_all[:, cols(c)].unsqueeze(1).to_broadcast([P, 2, D]),
                                    mv2[:, c.slot, 0:1], rstd2[:, c.slot:c.slot + 1], ALU.subtract, ALU.mult).then_inc(xn2_ready, 1)
                if n:
                    u = n.slot
                    dve.wait_ge(ln1_rstd, at(n, 1, 1))
                    wait(dve, qkT_ready, at(n, 1, -1))
                    V.tensor_scalar(by_head(xn[:, u, :]), x_all[:, cols(n)].rearrange("p (h d) -> p h d", d=HD), mv1[:, u, 0:1],
                                    rstd1[:, u:u + 1], ALU.subtract, ALU.mult).then_inc(xn_ready, 1)
                maximum(2)
                maximum(3)
                if r:
                    u = r.slot
                    dve.wait_ge(cum_ready, at(r, 1, 1))
                    wait(dve, carry_done, at(r))
                    V.tensor_tensor(place[:, :, :].rearrange("p k e -> p (k e)"), R_BANK[:, 64:64 + 2 * E], carry[:, 1 - u, :], ALU.add).then_inc(place_done, 1)
                    V.tensor_tensor(carry[:, u, :], R_BANK[:, 96:96 + 2 * E], carry[:, 1 - u, :], ALU.add).then_inc(carry_done, 1)
                    dve.wait_ge(place_done, at(r, 1, 1))
                    V.tensor_tensor(place2[:, :, :], place[:, :, :], chosen[:, u, :, :], ALU.mult).then_inc(picked, 1)
                    dve.wait_ge(picked, at(r, 1, 1))
                    V.tensor_reduce(pos[:, :], place2[:, :, :], AX.X, ALU.add).then_inc(pos_summed, 1)
                    dve.wait_ge(pos_summed, at(r, 1, 1))
                    V.tensor_tensor(pos2[:, :], pos[:, :], pos_sign[:, :], ALU.mult).then_inc(pos_signed, 1)
                    dve.wait_ge(pos_signed, at(r, 1, 1))
                    V.tensor_tensor(pos3[:, :], pos2[:, :], pos_base[:, :], ALU.add).then_inc(pos_based, 1)
                    dve.wait_ge(pos_based, at(r, 1, 1))
                    wait(dve, row_out[r.place], r.quad * 32)
                    V.scalar_tensor_tensor(out=slot_i[:, r.place, :], in0=idxf[:, r.slot, :], scalar=float(REGION), in1=pos3[:, :],
                                           op0=ALU.mult, op1=ALU.add).then_inc(slot_done, 1)

            pipeline(dve, step)

            dve.wait_ge(carry_done, B)
            last_carry = carry[0:1, (B - 1) % 2, :]
            link(V.tensor_scalar(n_first[:, :], last_carry[:, 0:E], float(CAP), None, ALU.min))
            link(V.tensor_scalar(n_room[:, :], n_first[:, :], -1.0, float(CAP), ALU.mult, ALU.add))
            link(V.tensor_tensor(n_second[:, :], last_carry[:, E:2 * E], n_room[:, :], ALU.min))
            link(V.tensor_tensor(n_kept[:, :], n_first[:, :], n_second[:, :], ALU.add))
            link(V.tensor_scalar(nt_i[:, :], n_kept[:, :], float(P - 1), None, ALU.add))
            link(V.tensor_scalar(nt_sh[:, :], nt_i[:, :], 7, None, ALU.logical_shift_right))
            link(V.tensor_copy(nt_f[:, :], nt_sh[:, :]))
            link(V.tensor_tensor(t_mul[:, :, :], earlier[:, :, :], nt_f[:, :].unsqueeze(1).to_broadcast([1, E, E]), ALU.mult))
            link(V.tensor_reduce(t_first[:, :], t_mul[:, :, :], AX.X, ALU.add))
            link(V.tensor_tensor(t_end[:, :], t_first[:, :], nt_f[:, :], ALU.add))
            link(V.tensor_tensor(r_start[:, :], region_i[:, :], n_second[:, :], ALU.subtract))
            link(V.tensor_tensor(pad_tab[:, :], r_start[:, :], n_kept[:, :], ALU.add))
            link(V.scalar_tensor_tensor(out=r_off[:, :], in0=t_first[:, :], scalar=float(-P), in1=r_start[:, :], op0=ALU.mult, op1=ALU.add))
            link(V.tensor_tensor(r_step[:, 0:E - 1], r_off[:, 1:E], r_off[:, 0:E - 1], ALU.subtract))
            link(V.tensor_tensor(past[:, :, :], tile_i[:, :].unsqueeze(2).to_broadcast([1, NT, E]),
                                 t_end[:, :].unsqueeze(1).to_broadcast([1, NT, E]), ALU.is_ge))
            link(V.tensor_reduce(tile_e[:, :], past[:, :, 0:E - 1], AX.X, ALU.add))
            link(V.tensor_copy(expert_tab[:, :], tile_e[:, :]))
            link(V.tensor_tensor(past_step[:, :, 0:E - 1], past[:, :, 0:E - 1],
                                 r_step[:, 0:E - 1].unsqueeze(1).to_broadcast([1, NT, E - 1]), ALU.mult))
            link(V.tensor_reduce(tile_r[:, :], past_step[:, :, 0:E - 1], AX.X, ALU.add))
            link(V.scalar_tensor_tensor(out=tile_r2[:, :], in0=tile_i[:, :], scalar=float(P), in1=tile_r[:, :], op0=ALU.mult, op1=ALU.add))
            link(V.tensor_scalar(tile_r3[:, :], tile_r2[:, :], r_off[:, 0:1], float(-PAD_ROW), ALU.add, ALU.add))
            link(V.tensor_scalar(tile_r[:, :], past[:, :, E - 1], -1.0, 1.0, ALU.mult, ALU.add))
            link(V.tensor_tensor(tile_r4[:, :], tile_r3[:, :], tile_r[:, :], ALU.mult))
            V.tensor_scalar(row_tab[:, :], tile_r4[:, :], float(PAD_ROW), None, ALU.add).then_inc(table_done, 1)

            V.tensor_tensor(tdiff[:, :, :], top_all[:, :, :], top_all[:, :, 0:1].to_broadcast([P, B, 8]), ALU.subtract).then_inc(gexp_ready, 1)
            dve.wait_ge(gexp_done, 1)
            link(V.tensor_reduce(gsum[:, :], texp[:, :, :], AX.X, ALU.add))
            link(V.tensor_scalar(gden[:, :], gsum[:, :], GATE_EPS, 1.0, ALU.mult, ALU.add))
            link(V.tensor_tensor(gden2[:, :], gden[:, :], texp[:, :, 1], ALU.add))
            link(V.reciprocal(grec[:, :], gden2[:, :]))
            link(V.tensor_scalar(gw[:, 0, :], grec[:, :], tanh_g[:, 1:2], None, ALU.mult))
            link(V.tensor_tensor(gw[:, 1, :], gw[:, 0, :], texp[:, :, 1], ALU.mult))

            dve.wait_ge(moe_loaded, 48)

            def early(i, v):
                t = i * 4 + v
                e = dve.value_load(expert_tab[0:1, bass.ds(t, 1)], min_val=0, max_val=E - 1)
                wait(dve, y_ready[v], i)
                wait(dve, hT_ready, t - 3)
                V.tensor_copy(ex_cur[:, v, :], ex_sb[:, bass.ds(e, 1), :].rearrange("p e f -> p (e f)")).then_inc(ex_ready, 1)
                wait(dve, xt_loaded[v], i * 16 + 16)
                wait(dve, y_out[v], i * 16)
                V.tensor_copy(dest[:, v, :], xt[:, v, D:D + 1].bitcast(U32)).then_inc(dest_ready, 1)
                dve.wait_ge(xt_psum, t + 1)
                V.tensor_copy(xtT[:, v % 2, :], X_BANK[v % 2][:, 0:P]).then_inc(xtT_ready, 1)

            def back(i, v):
                t = i * 4 + v
                dve.wait_ge(y_psum, t + 1)
                V.tensor_tensor(y_s[:, v, :], Y_BANK[v % 2][:, 0:D], ex_cur[:, v, FF:FF + D], ALU.add).then_inc(y_ready[v], 1)

            tiles(dve, early, lambda i, v: None, back)

            for k in range(NC):
                dve.wait_ge(yc_loaded[k], 16 * K)
                for s in range(CH * k, CH * k + CH):
                    xv = x_all[:, s * D:s * D + D]
                    V.scalar_tensor_tensor(out=xv, in0=yc[:, 0, s, :], scalar=gw[:, 0, s:s + 1], in1=xv, op0=ALU.mult, op1=ALU.add).then_inc(fin_step, 1)
                    dve.wait_ge(fin_step, s + 1)
                    V.scalar_tensor_tensor(out=xv, in0=yc[:, 1, s, :], scalar=gw[:, 1, s:s + 1], in1=xv, op0=ALU.mult, op1=ALU.add).then_inc(fin_done, 1)


_INS = ['x', 'ctx_1024', 'g_xattn', 'g_ffn', 'L0_xattn_w_out', 'L0_xattn_b_out', 'L0_ffn_Wg', 'L0_ffn_W1', 'L0_ffn_b1',
        'L0_ffn_W2', 'L0_ffn_b2']


def kernel(**inputs):
    import numpy as _np
    import concourse.bacc as _bacc
    from concourse import mybir as _mybir
    from concourse.bass_utils import run_bass_kernel_spmd as _run

    nc = _bacc.Bacc("TRN2", target_bir_lowering=False, num_devices=1)
    arrays, args = {}, []
    for name in _INS:
        a = _np.ascontiguousarray(inputs[name])
        arrays[f"in_{name}_dram"] = a
        args.append(nc.dram_tensor(f"in_{name}_dram", a.shape, _mybir.dt.from_np(a.dtype), kind="ExternalInput").ap())
    shape = inputs["x"].shape
    args.append(nc.dram_tensor("out_0_dram", shape, _mybir.dt.float32, kind="ExternalOutput").ap())
    flamingo_layer(nc, *args)
    r = _run(nc, [arrays], core_ids=[0])
    return r.results[0]["out_0_dram"]
```

```python
from collections import namedtuple
from contextlib import ExitStack

import concourse.bass as bass
from concourse import mybir

F32 = mybir.dt.float32
BF16 = mybir.dt.bfloat16
I32 = mybir.dt.int32
U32 = mybir.dt.uint32
ALU = mybir.AluOpType
ACT = mybir.ActivationFunctionType
AX = mybir.AxisListType

P = 128
HD = 8
LN_EPS = 1e-5
GATE_EPS = 1e-9

TERMS = (("low", "high"), ("middle", "high"), ("high", "high"), ("high", "middle"), ("high", "low"), ("middle", "middle"))


class Seq(namedtuple("Seq", "quad place")):

    @property
    def is_first(self):
        return isinstance(self.quad, int) and self.quad == 0 and self.place == 0

    @property
    def slot(self):
        return self.place % 2

    @property
    def pair(self):
        return self.quad * 2 + self.place // 2


def flamingo_layer(nc, x, ctx, g_xattn, g_ffn, w_out, b_out, Wg, W1, b1, W2, b2, out):
    B, S, D = x.shape
    E = Wg.shape[1]
    FF = W1.shape[2]
    T = B * S
    K = 2
    CAP = 2 * K * T // E
    H = D // HD
    G = 4
    J = H // G
    MAX_ROW = 96
    assert len(TERMS) * HD <= MAX_ROW
    SCALE = 1.0 / float(D) ** 0.5
    NF = FF // P
    MID = T
    REGION = 2 * T + P
    PAD_ROW = E * REGION
    NT = 72
    assert NT % 4 == 0 and NT * P > K * T + (E - 1) * (P - 1) and S == P and D == P
    ROW = D + 1
    NZ = K * T // (4 * P)
    assert NZ == 3 * 5 + 1
    CH = 4
    CHUNKS = (0, 2, 8, 14, 20, 26, B)
    NC = B // CH

    xs_dram = nc.dram_tensor("expert_rows", [PAD_ROW + P, ROW], F32, kind="Internal").ap()
    y_dram = nc.dram_tensor("choice_rows", [K * T, D], F32, kind="Internal").ap()

    with ExitStack() as es:
        def sb(name, shape, dt=F32):
            return es.enter_context(nc.sbuf_tensor(name, shape, dt))

        def sem(name):
            return es.enter_context(nc.semaphore(name))

        bank = [es.enter_context(nc.psum_tensor(f"bank{i}", [P, 512], F32)) for i in range(8)]

        col_i = sb("col_i", [P, P], I32)
        diff_i = sb("diff_i", [P, P], I32)
        ident = sb("ident", [P, P])
        ident_b = sb("ident_b", [P, P], BF16)
        before = sb("before", [P, 2, P], BF16)
        every = sb("every", [P, 2, P], BF16)
        neg_half = sb("neg_half", [P, 1])
        iota8 = sb("iota8", [P, 8])
        ids = sb("ids", [P, B, 2], I32)
        carry0 = sb("carry0", [P, 2 * E])
        zeros = sb("zeros", [P, 512])
        pad = sb("pad", [P, ROW])
        wout_sb = sb("wout_sb", [P, D])
        wout_p = sb("wout_p", [P, D])
        woutT = sb("woutT", [P, D])
        bias_out = sb("bias_out", [P, D])
        gates = sb("gates", [P, 2])
        tanh_g = sb("tanh_g", [P, 2])
        wg_sb = sb("wg_sb", [P, E])
        ED = FF + D + NF
        ex_sb = sb("ex_sb", [P, E, ED])
        w2_sb = sb("w2_sb", [P, E * NF * D])
        b1_rows = sb("b1_rows", [E * NF, P])
        x_all = sb("x_all", [P, B * D])
        ctx_all = sb("ctx_all", [P, B * D])
        st1 = sb("st1", [P, 2, 6])
        mv1 = sb("mv1", [P, 2, 2])
        ve1 = sb("ve1", [P, 2])
        rstd1 = sb("rstd1", [P, 2])
        st2 = sb("st2", [P, 2, 6])
        mv2 = sb("mv2", [P, 2, 2])
        ve2 = sb("ve2", [P, 2])
        rstd2 = sb("rstd2", [P, 2])
        xn = sb("xn", [P, 2, D])
        ctx_d = sb("ctx_d", [P, 2, D])
        parts = sb("parts", [P, 2, 2 * len(TERMS), P], BF16)
        rest = sb("rest", [P, 2, 2, P])
        stack = sb("stack", [P, 4, H, 2 * P], BF16)
        values = sb("values", [P, 2, 2, 2, G, 32])
        negmax = sb("negmax", [P, 2, H], BF16)
        mT = sb("mT", [H, 2, P], BF16)
        probs = sb("probs", [P, 2, G, J * P])
        oS = sb("oS", [P, 2, 2 * P])
        rsum = sb("rsum", [P, 2, H])
        attn = sb("attn", [P, 2, D])
        aT = sb("aT", [P, 2, P])
        xrow = sb("xrow", [P, 4, 2, ROW])
        xn2T = sb("xn2T", [P, 2, P])
        lg = sb("lg", [P, 2, E])
        top = sb("top", [P, 2, 8])
        topi = sb("topi", [P, 2, 8], U32)
        chosen = sb("chosen", [P, 2, 2, E], BF16)
        carry = sb("carry", [P, 2, 2 * E])
        place = sb("place", [P, 2, E])
        place2 = sb("place2", [P, 2, E])
        slot_i = sb("slot_i", [P, 4, 2], U32)
        top_all = sb("top_all", [P, B, 8])
        tdiff = sb("tdiff", [P, B, 8])
        texp = sb("texp", [P, B, 8])
        gsum = sb("gsum", [P, B])
        gden = sb("gden", [P, B])
        gden2 = sb("gden2", [P, B])
        gw = sb("gw", [P, 2, B])
        grec = sb("grec", [P, B])
        n_first = sb("n_first", [1, E])
        n_room = sb("n_room", [1, E])
        n_second = sb("n_second", [1, E])
        n_kept = sb("n_kept", [1, E])
        nt_i = sb("nt_i", [1, E], I32)
        nt_sh = sb("nt_sh", [1, E], I32)
        nt_f = sb("nt_f", [1, E])
        pair_i = sb("pair_i", [1, E, E], I32)
        earlier = sb("earlier", [1, E, E])
        t_mul = sb("t_mul", [1, E, E])
        t_first = sb("t_first", [1, E])
        t_end = sb("t_end", [1, E])
        placed = sb("placed", [1, 2 * E])
        r_start = sb("r_start", [1, E])
        r_off = sb("r_off", [1, E])
        r_step = sb("r_step", [1, E])
        tile_i = sb("tile_i", [1, NT])
        past = sb("past", [1, NT, E])
        past_step = sb("past_step", [1, NT, E])
        tile_e = sb("tile_e", [1, NT])
        tile_r = sb("tile_r", [1, NT])
        tile_r2 = sb("tile_r2", [1, NT])
        tile_r3 = sb("tile_r3", [1, NT])
        tile_r4 = sb("tile_r4", [1, NT])
        expert_tab = sb("expert_tab", [1, NT], I32)
        row_tab = sb("row_tab", [1, NT], I32)
        pad_tab = sb("pad_tab", [1, E], I32)
        xt = sb("xt", [P, 4, ROW])
        dest = sb("dest", [P, 4, 1], U32)
        xtT = sb("xtT", [P, 2, P])
        ex_cur = sb("ex_cur", [P, 4, ED])
        hT = sb("hT", [P, 2, NF, P])
        y_s = sb("y_s", [P, 4, D])
        yc = stack[:, :, :, :].rearrange("p s h q -> p (s h q)").bitcast(F32).rearrange("p (k b d) -> p k b d", k=K, b=B)

        S_BANK, E_BANK = bank[0:2], bank[2:4]
        TA = bank[4]
        TB = bank[5]
        O_BANK = bank[6]
        R_BANK = bank[7]
        PROJ, A_T = O_BANK[:, 256:256 + D], O_BANK[:, 384:384 + P]
        O_T = TA[:, 2 * P:4 * P].rearrange("p (x k) -> p x k", k=16)
        TB_max = TB[0:H, 256:256 + P // 2].bitcast(BF16)
        X_BANK, H_BANK, Y_BANK = bank[0:2], bank[2:4], bank[4:6]

        iota_done, const_done, chain = sem("iota_done"), sem("const_done"), sem("chain")
        pool_const = sem("pool_const")
        gate_loaded, w_loaded, moe_loaded = sem("gate_loaded"), sem("w_loaded"), sem("moe_loaded")
        x_loaded = [sem(f"x_loaded{k}") for k in range(len(CHUNKS) - 1)]
        ctx_loaded = [sem(f"ctx_loaded{k}") for k in range(len(CHUNKS) - 1)]
        wout_ordered = sem("wout_ordered")
        tanh_done, woutT_psum, b1T_psum, prep_done = sem("tanh_done"), sem("woutT_psum"), sem("b1T_psum"), sem("prep_done")
        zeroed = sem("zeroed")
        ctx_d_ready = sem("ctx_d_ready")
        stack_free = sem("stack_free")
        stack_ones = sem("stack_ones")
        stack_in = [sem(f"stack_in{u}") for u in range(2)]
        mT_in = [sem(f"mT_in{u}") for u in range(2)]
        ln1_stats, ln1_aggr, ln1_var, ln1_rstd, xn_ready = sem("ln1_stats"), sem("ln1_aggr"), sem("ln1_var"), sem("ln1_rstd"), sem("xn_ready")
        xb_done = sem("xb_done")
        qkT_ready, high_ready, rest_ready = sem("qkT_ready"), sem("high_ready"), sem("rest_ready")
        middle_ready, parts_ready, values_ready = sem("middle_ready"), sem("parts_ready"), sem("values_ready")
        oS_ready, oT_psum, attn_ready, attnT_psum = sem("oS_ready"), sem("oT_psum"), sem("attn_ready"), sem("attnT_psum")
        s_ready, max_done, m_psum, mT_ready = sem("s_ready"), sem("max_done"), sem("m_psum"), sem("mT_ready")
        e_ready, exp_done, o_ready = sem("e_ready"), sem("exp_done"), sem("o_ready")
        rsum_done, aT_ready, proj_ready = sem("rsum_done"), sem("aT_ready"), sem("proj_ready")
        x1_done, ln2_stats, ln2_aggr, ln2_var, ln2_rstd = sem("x1_done"), sem("ln2_stats"), sem("ln2_aggr"), sem("ln2_var"), sem("ln2_rstd")
        xn2_ready, xn2T_psum, xn2T_ready = sem("xn2_ready"), sem("xn2T_psum"), sem("xn2T_ready")
        logit_ready, lg_done, chosen_done = sem("logit_ready"), sem("lg_done"), sem("chosen_done")
        top_max, top_idx = sem("top_max"), sem("top_idx")
        cum_ready, slot_done = sem("cum_ready"), sem("slot_done")
        place_done, carry_done, picked, ids_done = sem("place_done"), sem("carry_done"), sem("picked"), sem("ids_done")
        row_out = [sem(f"row_out{u}") for u in range(4)]
        gexp_ready, gexp_done = sem("gexp_ready"), sem("gexp_done")
        pad_tab_done = sem("pad_tab_done")
        table_done, pads_out = sem("table_done"), sem("pads_out")
        xt_loaded = [sem(f"xt_loaded{v}") for v in range(4)]
        xt_psum, xtT_ready, ex_ready, dest_ready = sem("xt_psum"), sem("xtT_ready"), sem("ex_ready"), sem("dest_ready")
        h_psum, hT_ready, y_psum = sem("h_psum"), sem("hT_ready"), sem("y_psum")
        y_ready = [sem(f"y_ready{v}") for v in range(4)]
        y_out = [sem(f"y_out{v}") for v in range(4)]
        yc_loaded = [sem(f"yc_loaded{k}") for k in range(NC)]
        fin_step, fin_done = sem("fin_step"), sem("fin_done")
        stored = sem("stored")

        def at(s, scale=1, plus=0):
            return s.quad * (4 * scale) + (s.place * scale + plus)

        def wait(eng, semaphore, value):
            if isinstance(value, int) and value < 1:
                return
            eng.wait_ge(semaphore, value)

        def wait_alone(eng, semaphore, value):
            eng.wait_ge(const_done, 1)
            eng.wait_ge(semaphore, value)

        def cols(s, width=P):
            return bass.ds(at(s, width), width) if not isinstance(s.quad, int) else slice(at(s, width), at(s, width) + width)

        def chunks_due(s):
            return {0: [0], 2: [1], 8: range(2, len(CHUNKS) - 1)}.get(at(s), []) if isinstance(s.quad, int) else []

        def first_quad(s):
            return isinstance(s.quad, int) and s.quad == 0

        def by_head(columns):
            return columns.rearrange("p (d h) -> p h d", d=HD)

        def pipeline(eng, step):
            BEHIND = (1, 0, -2, -3, -4, -5, -6, -7, -8)

            def due(t):
                return [Seq(k // 4, k % 4) if 0 <= k < B else None for k in (t + k for k in BEHIND)]

            FIRST, LAST = 8, B - 4
            for t in range(-1, FIRST):
                step(*due(t))
            with eng.Fori(FIRST // 4, LAST // 4) as i:
                for u in range(4):
                    step(*[Seq(i + (u + k) // 4, (u + k) % 4) for k in BEHIND])
            for t in range(LAST, B - min(BEHIND)):
                step(*due(t))

        def write_pads(eng, experts):
            eng.wait_ge(pad_tab_done, 1)
            for u in range(4):
                eng.wait_ge(row_out[u], 32 * (B // 4))
            for e in experts:
                r = eng.value_load(pad_tab[0:1, e:e + 1], min_val=0, max_val=PAD_ROW)
                eng.dma_start(xs_dram[bass.ds(r, P), :], pad[:, :]).then_inc(pads_out, 16)

        def tiles(eng, early, front, back):
            NI = NT // 4

            def turn(i, v, ahead):
                for part, k in ((early, 2), (front, 1), (back, 0)):
                    if v + k < 4 or ahead:
                        part(i + (v + k) // 4, (v + k) % 4)

            early(0, 0)
            early(0, 1)
            front(0, 0)
            for v in range(4):
                turn(0, v, True)
            with eng.Fori(1, NI - 1) as i:
                for v in range(4):
                    turn(i, v, True)
            for v in range(4):
                turn(NI - 1, v, False)

        block = es.enter_context(nc.Block())

        @block.sync
        def _(sp):
            xv = x.rearrange("b s d -> s b d")
            xa = x_all[:, :].rearrange("p (b d) -> p b d", b=B)
            cv = ctx.rearrange("b s d -> s b d")
            ca = ctx_all[:, :].rearrange("p (b d) -> p b d", b=B)

            def load_sequences(k):
                part = slice(CHUNKS[k], CHUNKS[k + 1])
                sp.dma_start(xa[:, part, :], xv[:, part, :]).then_inc(x_loaded[k], 16)
                sp.dma_start(ca[:, part, :], cv[:, part, :]).then_inc(ctx_loaded[k], 16)

            load_sequences(0)
            sp.dma_start(gates[:, 0:1], g_xattn.partition_broadcast(P)).then_inc(gate_loaded, 16)
            sp.dma_start(gates[:, 1:2], g_ffn.partition_broadcast(P)).then_inc(gate_loaded, 16)
            sp.dma_start(wout_sb[:, :], w_out).then_inc(w_loaded, 16)
            sp.dma_start(bias_out[:, :], b_out.partition_broadcast(P)).then_inc(w_loaded, 16)
            sp.dma_start(b1_rows[:, :], b1.rearrange("e (c f) -> (e c) f", c=NF)).then_inc(w_loaded, 16)
            sp.dma_start(wg_sb[:, :], Wg).then_inc(w_loaded, 16)
            for k in range(1, len(CHUNKS) - 1):
                load_sequences(k)

            w1v = W1.rearrange("e d f -> d e f")
            w2v = W2.rearrange("e (c f) d -> f e c d", c=NF)
            w2s = w2_sb[:, :].rearrange("p (e c d) -> p e c d", e=E, c=NF)
            zrows = y_dram[0:K * T, :].rearrange("(k p r) d -> k p (r d)", p=P, r=4)

            def side_transfer(k):
                pair = slice(k // 2 * 2, k // 2 * 2 + 2)
                if k < E and k % 2 == 0:
                    sp.dma_start(ex_sb[:, pair, 0:FF], w1v[:, pair, :]).then_inc(moe_loaded, 16)
                elif k < E:
                    sp.dma_start(w2s[:, pair], w2v[:, pair]).then_inc(moe_loaded, 16)
                elif k == E:
                    sp.dma_start(ex_sb[:, :, FF:FF + D], b2.partition_broadcast(P)).then_inc(moe_loaded, 16)
                elif k == E + 1:
                    sp.dma_start(zrows[NZ - 1], zeros[:, :]).then_inc(zeroed, 16)

            sp.wait_ge(pool_const, 1)

            def step(n, a, m, b, p, q, c, r, d):
                if b:
                    sp.wait_ge(mT_ready, at(b, 1, 1))
                    sp.dma_start(stack[MAX_ROW:MAX_ROW + 1, b.place, :, 0:P], mT[:, b.slot, :]).then_inc(mT_in[b.slot], 16)
                if a:
                    sp.wait_ge(parts_ready, at(a, 1, 1))
                    sp.wait_ge(stack_free, at(a, 1, 1))
                    if first_quad(a):
                        sp.wait_ge(stack_ones, at(a, 1, 1))
                    for t in range(len(TERMS)):
                        sp.dma_start(stack[HD * t:HD * t + HD, a.place, :, :],
                                     parts[:, a.slot, 2 * t:2 * t + 2, :].rearrange("p b q -> p (b q)")).then_inc(stack_in[a.slot], 16)
                if a and not isinstance(a.quad, int):
                    if a.place < 3:
                        k = (a.quad - 2) * 3 + a.place
                        sp.dma_start(zrows[bass.ds(k, 1), :, :].rearrange("k p x -> (k p) x"), zeros[:, :]).then_inc(zeroed, 16)
                elif a and 1 <= at(a) < 8:
                    side_transfer(at(a) - 1)
                elif d and not a:
                    side_transfer(at(d) - (B - 8) + 7)

            pipeline(sp, step)
            write_pads(sp, range(0, E, 2))
            sp.dma_start(xs_dram[PAD_ROW:PAD_ROW + P, :], pad[:, :]).then_inc(pads_out, 16)
            sp.wait_ge(table_done, 1)
            first_rows = [sp.value_load(row_tab[0:1, v:v + 1], min_val=0, max_val=PAD_ROW) for v in range(4)]
            sp.wait_ge(pads_out, 16 * (E + 1))
            for v in range(4):
                sp.dma_start(xt[:, v, :], xs_dram[bass.ds(first_rows[v], P), :]).then_inc(xt_loaded[v], 16)

            def load_tile(i, v):
                t = i * 4 + v
                wait(sp, xt_psum, t - 3)
                wait(sp, dest_ready, t - 3)
                r = sp.value_load(row_tab[0:1, bass.ds(t, 1)], min_val=0, max_val=PAD_ROW)
                sp.dma_start(xt[:, v, :], xs_dram[bass.ds(r, P), :]).then_inc(xt_loaded[v], 16)

            with sp.Fori(1, NT // 4) as i:
                for v in range(4):
                    load_tile(i, v)

            for v in range(4):
                sp.wait_ge(y_out[v], 16 * (NT // 4))
            yv = y_dram[0:K * T, :].rearrange("(c b p) d -> c p b d", c=K, p=P)
            for k in range(NC):
                for c in range(K):
                    sp.dma_start(yc[:, c, CH * k:CH * k + CH, :], yv[c, :, CH * k:CH * k + CH, :]).then_inc(yc_loaded[k], 16)
            ov = out.rearrange("b s d -> s b d")
            for k in range(NC):
                sp.wait_ge(fin_done, CH * (k + 1))
                sp.dma_start(ov[:, CH * k:CH * k + CH, :], xa[:, CH * k:CH * k + CH, :]).then_inc(stored, 16)
            sp.wait_ge(stored, 16 * NC)

        @block.gpsimd
        def _(pool):
            nc.gpsimd.iota(col_i[:, :], [[1, P]], base=0, channel_multiplier=0)
            nc.gpsimd.iota(diff_i[:, :], [[1, P]], base=0, channel_multiplier=-1)
            nc.gpsimd.iota(ids[:, :, :], [[P, B], [T, 2]], base=0, channel_multiplier=1)
            nc.gpsimd.iota(pair_i[:, :, :], [[-1, E], [1, E]], base=0, channel_multiplier=0)
            nc.gpsimd.iota(tile_i[:, :], [[1, NT]], base=0, channel_multiplier=0, allow_small_or_imprecise_dtypes=True)
            nc.gpsimd.iota(pad[:, D:D + 1].bitcast(I32), [[0, 1]], base=K * T, channel_multiplier=1)
            nc.gpsimd.memset(pad[:, 0:D], 0.0)
            nc.gpsimd.memset(every[:, 0, :], 1.0)
            nc.gpsimd.memset(every[:, 1, :], -1.0)
            nc.gpsimd.memset(neg_half[:, :], -0.5)
            for t in (carry[:, 1, :], carry0[:, :]):
                last = nc.gpsimd.iota(t.rearrange("p (k e) -> p k e", k=2), [[-1, 2], [REGION, E]], base=MID, channel_multiplier=0,
                                      allow_small_or_imprecise_dtypes=True)
            last.then_inc(iota_done, 1)
            for j in range(2):
                nc.gpsimd.memset(values[:, :, :, j, :, 16 * (1 - j):16 * (2 - j)], 0.0)
                nc.gpsimd.memset(values[:, :, :, j, :, 16 * j + HD:16 * j + 16], 1.0)
            nc.gpsimd.memset(zeros[:, :], 0.0).then_inc(pool_const, 1)

            def step(n, a, m, b, p, q, c, r, d):
                if c:
                    pool.wait_ge(ln2_var, at(c, 1, 1))
                    nc.gpsimd.tensor_tensor(rstd2[:, c.slot:c.slot + 1], ve2[:, c.slot:c.slot + 1], neg_half[:, :],
                                            ALU.pow).then_inc(ln2_rstd, 1)
                    wait(pool, row_out[c.place], c.quad * 32)
                    nc.gpsimd.tensor_copy(xrow[:, c.place, :, D:D + 1].bitcast(I32),
                                          ids[:, bass.ds(at(c), 1), :].rearrange("p b k -> p (b k)").unsqueeze(2)).then_inc(ids_done, 1)
                if n:
                    pool.wait_ge(ln1_var, at(n, 1, 1))
                    nc.gpsimd.tensor_tensor(rstd1[:, n.slot:n.slot + 1], ve1[:, n.slot:n.slot + 1], neg_half[:, :],
                                            ALU.pow).then_inc(ln1_rstd, 1)
                if b:
                    if b.is_first:
                        pool.wait_ge(pool_const, 1)
                        pool.wait_ge(ctx_loaded[0], 16)
                    wait(pool, o_ready, at(b, 1, -1))
                    by_strip = ctx_all[:, cols(b)].rearrange("p (g s j d) -> p s g j d", g=G, s=2, j=2)
                    for j in range(2):
                        last = nc.gpsimd.tensor_copy(values[:, b.slot, :, j, :, 16 * j:16 * j + HD], by_strip[:, :, :, j, :])
                    last.then_inc(values_ready, 1)
                if a:
                    if a.is_first:
                        pool.wait_ge(prep_done, 3)
                    pool.wait_ge(xn_ready, at(a, 1, 1))
                    if d:
                        pool.wait_ge(slot_done, at(d, 1, 1))
                        pool.wait_ge(ids_done, at(d, 1, 1))
                    nc.gpsimd.tensor_tensor(x_all[:, cols(a)], x_all[:, cols(a)], bias_out[:, :], ALU.add).then_inc(xb_done, 1)
                if d:
                    if not a:
                        pool.wait_ge(slot_done, at(d, 1, 1))
                        pool.wait_ge(ids_done, at(d, 1, 1))
                    for k in range(2):
                        nc.gpsimd.indirect_dma_start(
                            xs_dram, bass.IndirectOffsetOnAxis(ap=slot_i[:, d.place, k:k + 1], axis=0),
                            xrow[:, d.place, k, :], None).then_inc(row_out[d.place], 16)
                if n and first_quad(n):
                    nc.gpsimd.memset(stack[:, n.place, :, P:2 * P], 1.0).then_inc(stack_ones, 1)

            pipeline(pool, step)

            pool.wait_ge(zeroed, 16 * NZ)

            last_row = pool.snap(K * T - 1)
            with pool.Fori(1, NT // 4 + 1) as i:
                for v in range(4):
                    wait_alone(pool, y_ready[v], i)
                    nc.gpsimd.indirect_dma_start(y_dram, bass.IndirectOffsetOnAxis(ap=dest[:, v, :], axis=0), y_s[:, v, :],
                                                 None, bounds_check=last_row, oob_is_err=False).then_inc(y_out[v], 16)

        @block.scalar
        def _(act):
            act.wait_ge(gate_loaded, 32)
            nc.scalar.activation(tanh_g[:, :], gates[:, :], ACT.Tanh).then_inc(tanh_done, 1)

            def step(n, a, m, b, p, q, c, r, d):
                if c:
                    act.wait_ge(attnT_psum, at(c, 1, 1))
                    wait(act, proj_ready, at(c, 1, -1))
                    nc.scalar.copy(aT[:, c.slot, :], A_T).then_inc(aT_ready, 1)
                if r:
                    act.wait_ge(xn2T_psum, at(r, 1, 1))
                    wait(act, logit_ready, at(r, 1, -1))
                    nc.scalar.copy(xn2T[:, r.slot, :], TB[:, P:2 * P]).then_inc(xn2T_ready, 1)
                if a:
                    act.wait_ge(qkT_ready, at(a, 1, 1))
                    wait(act, stack_in[a.slot], a.pair * (16 * len(TERMS)))
                    for o, blocks in ((0, slice(4, 9, 2)), (P, slice(1, 6, 2))):
                        last = nc.scalar.copy(parts[:, a.slot, blocks, :], TA[:, o:o + P].unsqueeze(1).to_broadcast([P, 3, P]))
                    last.then_inc(high_ready, 1)
                if b:
                    act.wait_ge(m_psum, at(b, 1, 1))
                    wait(act, mT_in[b.slot], b.pair * 16)
                    nc.scalar.copy(mT[:, b.slot, :], TB_max).then_inc(mT_ready, 1)
                if n:
                    for k in chunks_due(n):
                        act.wait_ge(ctx_loaded[k], 16)
                    wait(act, qkT_ready, at(n, 1, -1))
                    nc.scalar.copy(by_head(ctx_d[:, n.slot, :]), ctx_all[:, cols(n)].rearrange("p (h d) -> p h d", d=HD)).then_inc(ctx_d_ready, 1)
                if a:
                    act.wait_ge(rest_ready, at(a, 1, 1))
                    for o, blocks in ((0, slice(2, 11, 8)), (1, slice(7, 12, 4))):
                        last = nc.scalar.copy(parts[:, a.slot, blocks, :], rest[:, a.slot, o:o + 1, :].to_broadcast([P, 2, P]))
                    last.then_inc(middle_ready, 1)
                def exp(g):
                    if b:
                        act.wait_ge(e_ready, at(b, G, g + 1))
                        if g == 0:
                            wait(act, o_ready, at(b, 1, -1))
                        nc.scalar.activation(probs[:, b.slot, g, :], E_BANK[g % 2][:, :], ACT.Exp,
                                             scale=SCALE).then_inc(exp_done, 1)

                exp(0)
                exp(1)
                exp(2)
                if p:
                    act.wait_ge(o_ready, at(p, 1, 1))
                    wait(act, oT_psum, at(p, 1, -1))
                    nc.scalar.copy(oS[:, p.slot, :], O_BANK[:, 0:2 * P]).then_inc(oS_ready, 1)
                exp(3)

            pipeline(act, step)

            write_pads(act, range(1, E, 2))
            act.wait_ge(gexp_ready, 1)
            nc.scalar.activation(texp[:, :, :], tdiff[:, :, :], ACT.Exp).then_inc(gexp_done, 1)

            def gelu(i, v):
                t = i * 4 + v
                act.wait_ge(h_psum, t + 1)
                wait(act, y_psum, t - 1)
                for c in range(NF):
                    last = nc.scalar.activation(hT[:, v % 2, c, :], H_BANK[v % 2][:, c * P:c * P + P], ACT.Gelu,
                                                bias=ex_cur[:, v, FF + D + c:FF + D + c + 1])
                last.then_inc(hT_ready, 1)

            for v in range(4):
                gelu(0, v)
            with act.Fori(1, NT // 4) as i:
                for v in range(4):
                    gelu(i, v)

        @block.tensor
        def _(pe):
            pe.wait_ge(const_done, 1)
            pe.wait_ge(w_loaded, 64)
            pe.wait_ge(wout_ordered, 1)
            nc.tensor.transpose(TA[:, 0:P], wout_p[:, :], ident[:, :]).then_inc(woutT_psum, 1)
            nc.tensor.transpose(TB[:, 0:E * NF], b1_rows[:, :], ident[0:E * NF, 0:E * NF]).then_inc(b1T_psum, 1)
            pe.wait_ge(prep_done, 3)

            def step(n, a, m, b, p, q, c, r, d):
                def main_scores(g):
                    if not b:
                        return
                    if g == 0:
                        pe.wait_ge(mT_in[b.slot], b.pair * 16 + 16)
                    wait(pe, exp_done, at(b, G, g - 1))
                    for j in range(J):
                        head = stack[:, b.place, J * g + j, :]
                        last = nc.tensor.matmul(E_BANK[g % 2][:, j * P:j * P + P], head[:, P:2 * P], head[:, 0:P],
                                                start=True, stop=True)
                    last.then_inc(e_ready, 1)

                def max_scores(g):
                    if not m:
                        return
                    if g == 0:
                        pe.wait_ge(stack_in[m.slot], (m.pair + 1) * (16 * len(TERMS)))
                    wait(pe, max_done, at(m, G, g - 1))
                    for j in range(J):
                        head = stack[0:MAX_ROW, m.place, J * g + j, :]
                        last = nc.tensor.matmul(S_BANK[g % 2][:, j * P:j * P + P], head[:, 0:P], head[:, P:2 * P],
                                                start=True, stop=True)
                        if b and g == 3 and j == 0:
                            last.then_inc(stack_free, 1)
                    last.then_inc(s_ready, 1)

                def sums(h2):
                    if not p:
                        return
                    if h2 == 0:
                        pe.wait_ge(exp_done, at(p, G, G))
                        pe.wait_ge(values_ready, at(p, 1, 1))
                        if c:
                            pe.wait_ge(x1_done, at(c, 1, 1))
                        wait(pe, oS_ready, at(p))
                    for j in range(2):
                        head = (2 * h2 + j) * P
                        for g in range(G):
                            last = nc.tensor.matmul(O_BANK[32 * g:32 * g + 32, h2 * P:h2 * P + P], values[:, p.slot, h2, j, g, :],
                                                    probs[:, p.slot, g, head:head + P],
                                                    start=(j == 0), stop=(j == 1), skip_group_check=True)
                    if h2 == 1:
                        last.then_inc(o_ready, 1)

                if c:
                    pe.wait_ge(attn_ready, at(c, 1, 1))
                    pe.wait_ge(oS_ready, at(q, 1, 1) if q else B)
                    nc.tensor.transpose(A_T, attn[:, c.slot, :], ident[:, :]).then_inc(attnT_psum, 1)
                if r:
                    pe.wait_ge(xn2_ready, at(r, 1, 1))
                    wait(pe, mT_ready, at(b) if b else B)
                    nc.tensor.transpose(TB[:, P:2 * P], xrow[:, r.place, 0, 0:D], ident[:, :]).then_inc(xn2T_psum, 1)
                if a:
                    pe.wait_ge(ctx_d_ready, at(a, 1, 1))
                    pe.wait_ge(xn_ready, at(a, 1, 1))
                    wait(pe, rest_ready, at(a))
                    if q:
                        wait(pe, attn_ready, at(q))
                    nc.tensor.transpose(TA[:, 0:P], xn[:, a.slot, :], ident[:, :])
                    nc.tensor.transpose(TA[:, P:2 * P], ctx_d[:, a.slot, :], ident[:, :]).then_inc(qkT_ready, 1)
                max_scores(0)
                if b:
                    pe.wait_ge(max_done, at(b, G, G))
                    if r:
                        pe.wait_ge(xn2T_ready, at(r, 1, 1))
                    nc.tensor.transpose(TB_max, negmax[:, b.slot, :], ident_b[:, :]).then_inc(m_psum, 1)
                if c:
                    pe.wait_ge(aT_ready, at(c, 1, 1))
                    nc.tensor.matmul(PROJ, aT[:, c.slot, :], woutT[:, :], start=True, stop=True).then_inc(proj_ready, 1)
                max_scores(1)
                if r:
                    pe.wait_ge(xn2T_ready, at(r, 1, 1))
                    wait(pe, slot_done, at(r))
                    nc.tensor.matmul(R_BANK[:, 0:E], xn2T[:, r.slot, :], wg_sb[:, :], start=True, stop=True).then_inc(logit_ready, 1)
                if q:
                    pe.wait_ge(oS_ready, at(q, 1, 1))
                    wait(pe, rest_ready, at(a, 1, 1) if a else B)
                    wait(pe, attn_ready, at(q))
                    for h2 in range(2):
                        last = nc.tensor.transpose(TA[:, (2 + h2) * P:(3 + h2) * P], oS[:, q.slot, h2 * P:h2 * P + P], ident[:, :])
                    last.then_inc(oT_psum, 1)
                sums(0)
                sums(1)
                main_scores(0)
                main_scores(1)
                main_scores(2)
                max_scores(2)
                if r:
                    pe.wait_ge(chosen_done, at(r, 1, 1))
                    pe.wait_ge(lg_done, at(r, 1, 1))
                    for k in range(2):
                        nc.tensor.matmul(R_BANK[:, 64 + k * E:64 + k * E + E], before[:, k, :], chosen[:, r.slot, k, :], start=True, stop=True)
                        last = nc.tensor.matmul(R_BANK[:, 96 + k * E:96 + k * E + E], every[:, k, :], chosen[:, r.slot, k, :], start=True, stop=True)
                    last.then_inc(cum_ready, 1)
                main_scores(3)
                max_scores(3)

            pipeline(pe, step)

            pe.wait_ge(table_done, 1)
            pe.wait_ge(moe_loaded, 16 * 9)

            def early(i, v):
                t = i * 4 + v
                pe.wait_ge(xt_loaded[v], i * 16 + 16)
                wait(pe, xtT_ready, t - 1)
                nc.tensor.transpose(X_BANK[v % 2][:, 0:P], xt[:, v, 0:D], ident[:, :]).then_inc(xt_psum, 1)

            def front(i, v):
                t = i * 4 + v
                pe.wait_ge(xtT_ready, t + 1)
                pe.wait_ge(ex_ready, t + 1)
                wait(pe, hT_ready, t - 1)
                for c in range(NF):
                    last = nc.tensor.matmul(H_BANK[v % 2][:, c * P:c * P + P], ex_cur[:, v, c * P:c * P + P],
                                            xtT[:, v % 2, :], start=True, stop=True)
                last.then_inc(h_psum, 1)

            def back(i, v):
                t = i * 4 + v
                e = pe.value_load(expert_tab[0:1, bass.ds(t, 1)], min_val=0, max_val=E - 1)
                pe.wait_ge(hT_ready, t + 1)
                if v >= 2:
                    pe.wait_ge(y_ready[v - 2], i + 1)
                else:
                    wait(pe, y_ready[v + 2], i)
                for c in range(NF):
                    last = nc.tensor.matmul(Y_BANK[v % 2][:, 0:D], hT[:, v % 2, c, :],
                                            w2_sb[:, bass.ds(e * (NF * D) + c * D, D)], start=(c == 0), stop=(c == NF - 1))
                last.then_inc(y_psum, 1)

            tiles(pe, early, front, back)

        @block.vector
        def _(dve):
            links = [0]

            def link(ins):
                links[0] += 1
                ins.then_inc(chain, 1)
                dve.wait_ge(chain, links[0])

            dve.wait_ge(iota_done, 1)
            V = nc.vector
            V.tensor_scalar(ident[:, :], diff_i[:, :], 0.0, None, ALU.is_equal)
            V.tensor_scalar(ident_b[:, :], diff_i[:, :], 0.0, None, ALU.is_equal)
            V.tensor_scalar(before[:, 0, :], diff_i[:, :], 0.0, None, ALU.is_gt)
            V.tensor_scalar(before[:, 1, :], diff_i[:, :], 0.0, -1.0, ALU.is_gt, ALU.mult)
            V.tensor_copy(iota8[:, :], col_i[:, 0:8])
            V.tensor_scalar(earlier[:, :, :], pair_i[:, :, :], 0.0, None, ALU.is_lt).then_inc(const_done, 1)
            dve.wait_ge(const_done, 1)
            dve.wait_ge(tanh_done, 1)
            dve.wait_ge(w_loaded, 64)
            V.tensor_copy(wout_p[:, :].rearrange("p (s g k) -> p s g k", s=2, g=G),
                          wout_sb[:, :].rearrange("p (g s k) -> p s g k", s=2, g=G)).then_inc(wout_ordered, 1)
            dve.wait_ge(woutT_psum, 1)
            V.tensor_scalar(woutT[:, :], TA[:, 0:P], tanh_g[:, 0:1], None, ALU.mult).then_inc(prep_done, 1)
            V.tensor_scalar(bias_out[:, :], bias_out[:, :], tanh_g[:, 0:1], None, ALU.mult).then_inc(prep_done, 1)
            dve.wait_ge(b1T_psum, 1)
            V.tensor_copy(ex_sb[:, :, FF + D:ED], TB[:, 0:E * NF].rearrange("p (e c) -> p e c", e=E)).then_inc(prep_done, 1)

            def ln_aggr(mv, st, ve, u, aggr_sem, count, var_sem):
                V.bn_aggr(mv[:, u, :], st[:, u, :]).then_inc(aggr_sem, 1)
                dve.wait_ge(aggr_sem, count)
                V.tensor_scalar(ve[:, u:u + 1], mv[:, u, 1:2], LN_EPS, None, ALU.add).then_inc(var_sem, 1)

            def step(n, a, m, b, p, q, c, r, d):
                def maximum(g):
                    if m:
                        dve.wait_ge(s_ready, at(m, G, g + 1))
                        if g == 0:
                            wait(dve, m_psum, at(m, 1, -1))
                        V.tensor_reduce(negmax[:, m.slot, J * g:J * g + J], S_BANK[g % 2][:, :].rearrange("p (j k) -> p j k", j=J),
                                        AX.X, ALU.max, negate=True).then_inc(max_done, 1)

                maximum(0)
                if c:
                    u = c.slot
                    dve.wait_ge(proj_ready, at(c, 1, 1))
                    dve.wait_ge(xb_done, at(c, 1, 1))
                    V.tensor_tensor(x_all[:, cols(c)], PROJ, x_all[:, cols(c)], ALU.add).then_inc(x1_done, 1)
                if a:
                    u = a.slot
                    dve.wait_ge(high_ready, at(a, 1, 1))
                    wait(dve, parts_ready, at(a, 1, -1))
                    if c:
                        dve.wait_ge(x1_done, at(c, 1, 1))
                    V.tensor_tensor(rest[:, u, :, :], TA[:, 0:2 * P].rearrange("p (o q) -> p o q", o=2), parts[:, u, 4:6, :],
                                    ALU.subtract).then_inc(rest_ready, 1)
                if c:
                    if not a:
                        dve.wait_ge(x1_done, at(c, 1, 1))
                    V.bn_stats(st2[:, c.slot, :], x_all[:, cols(c)]).then_inc(ln2_stats, 1)
                if n:
                    for k in chunks_due(n):
                        dve.wait_ge(x_loaded[k], 16)
                    V.bn_stats(st1[:, n.slot, :], x_all[:, cols(n)]).then_inc(ln1_stats, 1)
                if c:
                    wait_alone(dve, ln2_stats, at(c, 1, 1))
                    ln_aggr(mv2, st2, ve2, c.slot, ln2_aggr, at(c, 1, 1), ln2_var)
                maximum(1)
                if r:
                    u = r.slot
                    dve.wait_ge(logit_ready, at(r, 1, 1))
                    if n:
                        dve.wait_ge(ln1_stats, at(n, 1, 1))
                    V.tensor_copy(lg[:, u, :], R_BANK[:, 0:E]).then_inc(lg_done, 1)
                if n:
                    if not r:
                        dve.wait_ge(ln1_stats, at(n, 1, 1))
                    ln_aggr(mv1, st1, ve1, n.slot, ln1_aggr, at(n, 1, 1), ln1_var)
                if r:
                    u = r.slot
                    wait_alone(dve, lg_done, at(r, 1, 1))
                    V.max(top[:, u, :], lg[:, u, :]).then_inc(top_max, 1)
                if a:
                    dve.wait_ge(middle_ready, at(a, 1, 1))
                    V.tensor_tensor(parts[:, a.slot, 0:10:9, :], rest[:, a.slot, :, :], parts[:, a.slot, 10:12, :],
                                    ALU.subtract).then_inc(parts_ready, 1)
                if r:
                    wait_alone(dve, top_max, at(r, 1, 1))
                    V.max_index(topi[:, u, :], top[:, u, :], lg[:, u, :]).then_inc(top_idx, 1)
                    V.tensor_copy(top_all[:, bass.ds(at(r), 1), :], top[:, u, :].unsqueeze(1))
                if q:
                    dve.wait_ge(oT_psum, at(q, 1, 1))
                    V.reciprocal(rsum[:, q.slot, :], O_T[:, :, HD]).then_inc(rsum_done, 1)
                if r:
                    dve.wait_ge(top_idx, at(r, 1, 1))
                if q:
                    dve.wait_ge(rsum_done, at(q, 1, 1))
                    wait(dve, attnT_psum, at(q, 1, -1))
                    V.tensor_tensor(attn[:, q.slot, :].rearrange("p (x k) -> p x k", k=HD), O_T[:, :, 0:HD],
                                    rsum[:, q.slot, :].unsqueeze(2).to_broadcast([P, H, HD]), ALU.mult).then_inc(attn_ready, 1)
                if r:
                    u = r.slot
                    V.tensor_tensor(chosen[:, u, :, :], iota8[:, :].unsqueeze(1).to_broadcast([P, 2, E]),
                                    topi[:, u, 0:2].unsqueeze(2).to_broadcast([P, 2, E]), ALU.is_equal).then_inc(chosen_done, 1)
                if c:
                    wait(dve, row_out[c.place], c.quad * 32)
                    dve.wait_ge(ln2_rstd, at(c, 1, 1))
                    V.tensor_scalar(xrow[:, c.place, :, 0:D], x_all[:, cols(c)].unsqueeze(1).to_broadcast([P, 2, D]),
                                    mv2[:, c.slot, 0:1], rstd2[:, c.slot:c.slot + 1], ALU.subtract, ALU.mult).then_inc(xn2_ready, 1)
                if n:
                    u = n.slot
                    dve.wait_ge(ln1_rstd, at(n, 1, 1))
                    wait(dve, qkT_ready, at(n, 1, -1))
                    V.tensor_scalar(by_head(xn[:, u, :]), x_all[:, cols(n)].rearrange("p (h d) -> p h d", d=HD), mv1[:, u, 0:1],
                                    rstd1[:, u:u + 1], ALU.subtract, ALU.mult).then_inc(xn_ready, 1)
                maximum(2)
                if r:
                    u = r.slot
                    dve.wait_ge(cum_ready, at(r, 1, 1))
                    wait(dve, carry_done, at(r))
                    V.tensor_tensor(place[:, :, :].rearrange("p k e -> p (k e)"), R_BANK[:, 64:64 + 2 * E], carry[:, 1 - u, :], ALU.add).then_inc(place_done, 1)
                    V.tensor_tensor(carry[:, u, :], R_BANK[:, 96:96 + 2 * E], carry[:, 1 - u, :], ALU.add).then_inc(carry_done, 1)
                    dve.wait_ge(place_done, at(r, 1, 1))
                    V.tensor_tensor(place2[:, :, :], place[:, :, :], chosen[:, u, :, :], ALU.mult).then_inc(picked, 1)
                maximum(3)
                if r:
                    dve.wait_ge(picked, at(r, 1, 1))
                    wait(dve, row_out[r.place], r.quad * 32)
                    with nc.allow_low_precision("one number that isn't zero, a whole one"):
                        V.tensor_reduce(slot_i[:, r.place, :], place2[:, :, :], AX.X, ALU.add).then_inc(slot_done, 1)
                if n and first_quad(n):
                    V.memset(stack[:, n.place, :, 0:P], 0.0).then_inc(stack_free, 1)

            pipeline(dve, step)

            V.tensor_tensor(tdiff[:, :, :], top_all[:, :, :], top_all[:, :, 0:1].to_broadcast([P, B, 8]), ALU.subtract).then_inc(gexp_ready, 1)

            dve.wait_ge(carry_done, B)
            last_carry = carry[0:1, (B - 1) % 2, :]
            V.tensor_tensor(placed[:, 0:E], last_carry[:, 0:E], carry0[0:1, 0:E], ALU.subtract)
            link(V.tensor_tensor(placed[:, E:2 * E], carry0[0:1, E:2 * E], last_carry[:, E:2 * E], ALU.subtract))
            link(V.tensor_scalar(n_first[:, :], placed[:, 0:E], float(CAP), None, ALU.min))
            link(V.tensor_scalar(n_room[:, :], n_first[:, :], -1.0, float(CAP), ALU.mult, ALU.add))
            link(V.tensor_tensor(n_second[:, :], placed[:, E:2 * E], n_room[:, :], ALU.min))
            link(V.tensor_tensor(n_kept[:, :], n_first[:, :], n_second[:, :], ALU.add))
            link(V.tensor_tensor(r_start[:, :], carry0[0:1, 0:E], n_second[:, :], ALU.subtract))
            V.tensor_tensor(pad_tab[:, :], r_start[:, :], n_kept[:, :], ALU.add).then_inc(pad_tab_done, 1)
            link(V.tensor_scalar(nt_i[:, :], n_kept[:, :], float(P - 1), None, ALU.add))
            link(V.tensor_scalar(nt_sh[:, :], nt_i[:, :], 7, None, ALU.logical_shift_right))
            link(V.tensor_copy(nt_f[:, :], nt_sh[:, :]))
            link(V.tensor_tensor(t_mul[:, :, :], earlier[:, :, :], nt_f[:, :].unsqueeze(1).to_broadcast([1, E, E]), ALU.mult))
            link(V.tensor_reduce(t_first[:, :], t_mul[:, :, :], AX.X, ALU.add))
            link(V.tensor_tensor(t_end[:, :], t_first[:, :], nt_f[:, :], ALU.add))
            link(V.scalar_tensor_tensor(out=r_off[:, :], in0=t_first[:, :], scalar=float(-P), in1=r_start[:, :], op0=ALU.mult, op1=ALU.add))
            link(V.tensor_tensor(r_step[:, 0:E - 1], r_off[:, 1:E], r_off[:, 0:E - 1], ALU.subtract))
            link(V.tensor_tensor(past[:, :, :], tile_i[:, :].unsqueeze(2).to_broadcast([1, NT, E]),
                                 t_end[:, :].unsqueeze(1).to_broadcast([1, NT, E]), ALU.is_ge))
            link(V.tensor_reduce(tile_e[:, :], past[:, :, 0:E - 1], AX.X, ALU.add))
            link(V.tensor_copy(expert_tab[:, :], tile_e[:, :]))
            link(V.tensor_tensor(past_step[:, :, 0:E - 1], past[:, :, 0:E - 1],
                                 r_step[:, 0:E - 1].unsqueeze(1).to_broadcast([1, NT, E - 1]), ALU.mult))
            link(V.tensor_reduce(tile_r[:, :], past_step[:, :, 0:E - 1], AX.X, ALU.add))
            link(V.scalar_tensor_tensor(out=tile_r2[:, :], in0=tile_i[:, :], scalar=float(P), in1=tile_r[:, :], op0=ALU.mult, op1=ALU.add))
            link(V.tensor_scalar(tile_r3[:, :], tile_r2[:, :], r_off[:, 0:1], float(-PAD_ROW), ALU.add, ALU.add))
            link(V.tensor_scalar(tile_r[:, :], past[:, :, E - 1], -1.0, 1.0, ALU.mult, ALU.add))
            link(V.tensor_tensor(tile_r4[:, :], tile_r3[:, :], tile_r[:, :], ALU.mult))
            V.tensor_scalar(row_tab[:, :], tile_r4[:, :], float(PAD_ROW), None, ALU.add).then_inc(table_done, 1)

            dve.wait_ge(moe_loaded, 16 * 9)

            def early(i, v):
                t = i * 4 + v
                e = dve.value_load(expert_tab[0:1, bass.ds(t, 1)], min_val=0, max_val=E - 1)
                wait(dve, y_ready[v], i)
                wait(dve, hT_ready, t - 3)
                V.tensor_copy(ex_cur[:, v, :], ex_sb[:, bass.ds(e, 1), :].rearrange("p e f -> p (e f)")).then_inc(ex_ready, 1)
                wait(dve, xt_loaded[v], i * 16 + 16)
                wait(dve, y_out[v], i * 16)
                V.tensor_copy(dest[:, v, :], xt[:, v, D:D + 1].bitcast(U32)).then_inc(dest_ready, 1)
                dve.wait_ge(xt_psum, t + 1)
                V.tensor_copy(xtT[:, v % 2, :], X_BANK[v % 2][:, 0:P]).then_inc(xtT_ready, 1)

            def back(i, v):
                t = i * 4 + v
                dve.wait_ge(y_psum, t + 1)
                V.tensor_tensor(y_s[:, v, :], Y_BANK[v % 2][:, 0:D], ex_cur[:, v, FF:FF + D], ALU.add).then_inc(y_ready[v], 1)

            tiles(dve, early, lambda i, v: None, back)

            dve.wait_ge(gexp_done, 1)
            link(V.tensor_reduce(gsum[:, :], texp[:, :, :], AX.X, ALU.add))
            link(V.tensor_scalar(gden[:, :], gsum[:, :], GATE_EPS, 1.0, ALU.mult, ALU.add))
            link(V.tensor_tensor(gden2[:, :], gden[:, :], texp[:, :, 1], ALU.add))
            link(V.reciprocal(grec[:, :], gden2[:, :]))
            link(V.tensor_scalar(gw[:, 0, :], grec[:, :], tanh_g[:, 1:2], None, ALU.mult))
            link(V.tensor_tensor(gw[:, 1, :], gw[:, 0, :], texp[:, :, 1], ALU.mult))

            for k in range(NC):
                dve.wait_ge(yc_loaded[k], 16 * K)
                for s in range(CH * k, CH * k + CH):
                    xv = x_all[:, s * D:s * D + D]
                    V.scalar_tensor_tensor(out=xv, in0=yc[:, 0, s, :], scalar=gw[:, 0, s:s + 1], in1=xv, op0=ALU.mult, op1=ALU.add).then_inc(fin_step, 1)
                    dve.wait_ge(fin_step, s + 1)
                    V.scalar_tensor_tensor(out=xv, in0=yc[:, 1, s, :], scalar=gw[:, 1, s:s + 1], in1=xv, op0=ALU.mult, op1=ALU.add).then_inc(fin_done, 1)


_INS = ['x', 'ctx_1024', 'g_xattn', 'g_ffn', 'L0_xattn_w_out', 'L0_xattn_b_out', 'L0_ffn_Wg', 'L0_ffn_W1', 'L0_ffn_b1',
        'L0_ffn_W2', 'L0_ffn_b2']


def kernel(**inputs):
    import numpy as _np
    import concourse.bacc as _bacc
    from concourse import mybir as _mybir
    from concourse.bass_utils import run_bass_kernel_spmd as _run

    nc = _bacc.Bacc("TRN2", target_bir_lowering=False, num_devices=1)
    arrays, args = {}, []
    for name in _INS:
        a = _np.ascontiguousarray(inputs[name])
        arrays[f"in_{name}_dram"] = a
        args.append(nc.dram_tensor(f"in_{name}_dram", a.shape, _mybir.dt.from_np(a.dtype), kind="ExternalInput").ap())
    shape = inputs["x"].shape
    args.append(nc.dram_tensor("out_0_dram", shape, _mybir.dt.float32, kind="ExternalOutput").ap())
    flamingo_layer(nc, *args)
    r = _run(nc, [arrays], core_ids=[0])
    return r.results[0]["out_0_dram"]
```
